# Optimizing a Trainium2 kernel written in Bass

```python
import numpy as np
import jax
import jax.numpy as jnp

def _softmax(x, axis=-1):
    return jax.nn.softmax(x, axis=axis)

def _gelu(x):
    return jax.nn.gelu(x, approximate=True)

def _silu(x):
    return jax.nn.silu(x)

def _sigmoid(x):
    return jax.nn.sigmoid(x)

def _layernorm(x, axis=-1, eps=1e-05):
    m = jnp.mean(x, axis=axis, keepdims=True)
    v = jnp.var(x, axis=axis, keepdims=True)
    return (x - m) / jnp.sqrt(v + eps)

def _scatter_add(tgt, idx, src, axis=0):
    return tgt.at[idx].add(src)

def _segment_sum(src, seg, n):
    return jax.ops.segment_sum(src, seg, n)
kernel_name = 'mk_adaln_ffn_d1_seqx_r8_2c72b3'

def setup_inputs(seed: int=0):
    np.random.seed(seed)
    _w = jnp.asarray

    def _rec_inputs():
        import jax
        import jax.numpy as jnp
        _rk = jax.random.key(seed)
        x = 7.22e-05 + 1 * jax.random.normal(jax.random.fold_in(_rk, 1), (32, 128, 128), jnp.float32)
        _lenS = 128 - jax.random.randint(jax.random.fold_in(_rk, 7), (32,), 0, max(1, 128 // 4) + 1, jnp.int32)
        _lenS2 = 128 - jax.random.randint(jax.random.fold_in(_rk, 8), (32,), 0, max(1, 128 // 4) + 1, jnp.int32)
        fside_BxSxS_0 = 4.13588e-05 + 0.999923 * jax.random.normal(jax.random.fold_in(_rk, 11), (32, 128, 128), jnp.float32)
        itok_B_18_1004 = jax.random.randint(jax.random.fold_in(_rk, 12), (32,), 18, 1005, jnp.int32)
        return (x, fside_BxSxS_0, itok_B_18_1004)
    x, fside_BxSxS_0, itok_B_18_1004 = _rec_inputs()

    def _L0_cond_setup():
        import jax, jax.numpy as jnp
        import numpy as np
        B, L1, L2, DIN, DOUT, H = (8, 128, 128, 128, 128, 16)
        DH = DOUT // H
        SCALE = 1.0 / np.sqrt(DH).astype(np.float32)
        key = jax.random.key(seed)
        ks = jax.random.split(key, 13)
        s = 0.02
        return {'seq1': jax.random.normal(ks[0], (B, L1, DIN), jnp.float32), 'seq2': jax.random.normal(ks[1], (B, L2, DIN), jnp.float32), 'seq_len1': jax.random.randint(ks[2], (B,), 1, L1 + 1, jnp.int32), 'Wq': jax.random.normal(ks[3], (DIN, DOUT), jnp.float32) * s, 'bq': jnp.zeros((DOUT,), jnp.float32), 'Wk': jax.random.normal(ks[4], (DIN, DOUT), jnp.float32) * s, 'bk': jnp.zeros((DOUT,), jnp.float32), 'Wv': jax.random.normal(ks[5], (DIN, DOUT), jnp.float32) * s, 'bv': jnp.zeros((DOUT,), jnp.float32), 'Wo': jax.random.normal(ks[6], (DOUT, DOUT), jnp.float32) * s, 'bo': jnp.zeros((DOUT,), jnp.float32), 'b_prev': jax.random.normal(ks[7], (1, 1, DIN), jnp.float32) * s, 'b_self': jax.random.normal(ks[8], (1, 1, DIN), jnp.float32) * s}
    _L0_cond_all = _L0_cond_setup()
    _L0_cond_in = {k: v for k, v in _L0_cond_all.items() if k in ('Wq', 'bq', 'Wk', 'bk', 'Wv', 'bv', 'Wo', 'bo', 'b_prev', 'b_self')}
    del _L0_cond_all

    def _L0_ffn_setup():
        import jax, jax.numpy as jnp
        import numpy as np
        DIM = 128
        DEPTH = 6
        HEADS = 16
        DIM_HEAD = 64
        WINDOW = 32
        INNER = HEADS * DIM_HEAD
        DIM_INNER = int(DIM * 4 * 2 / 3)
        QK_SCALE = 8.0

        def shift_tokens(t):
            a, s = jnp.split(t, 2, -1)
            s = jnp.pad(s, ((0, 0), (1, 0), (0, 0)))[:, :-1]
            return jnp.concatenate([a, s], -1)

        def l2norm(t):
            return t / jnp.maximum(jnp.linalg.norm(t, axis=-1, keepdims=True), 1e-12)

        def rotate_half(x):
            x1, x2 = jnp.split(x, 2, -1)
            return jnp.concatenate([-x2, x1], -1)

        def rotary_tables(n):
            half = jnp.arange(0, DIM_HEAD, 2, dtype=jnp.float32)
            inv_freq = 1.0 / 10000.0 ** (half / DIM_HEAD)
            t = jnp.arange(n, dtype=jnp.float32)
            freqs = t[:, None] * inv_freq[None, :]
            freqs = jnp.concatenate([freqs, freqs], -1)
            base_scale = (half + 0.4 * DIM_HEAD) / (1.4 * DIM_HEAD)
            power = (t - n // 2) / (WINDOW // 2)
            scale = base_scale[None, :] ** power[:, None]
            scale = jnp.concatenate([scale, scale], -1)
            return (freqs, scale)

        def local_attention(q, k, v):
            b, h, n, d = q.shape
            w = WINDOW
            nw = n // w
            bq = q.reshape(b, h, nw, w, d)
            bk = k.reshape(b, h, nw, w, d)
            bv = v.reshape(b, h, nw, w, d)

            def look(t):
                p = jnp.pad(t, ((0, 0), (0, 0), (1, 0), (0, 0), (0, 0)))
                return jnp.concatenate([p[:, :, :nw], p[:, :, 1:]], axis=3)
            bk2, bv2 = (look(bk), look(bv))
            seq = jnp.arange(n).reshape(nw, w)
            seq_p = jnp.pad(seq, ((1, 0), (0, 0)), constant_values=-1)
            jt = jnp.concatenate([seq_p[:nw], seq_p[1:]], axis=1)
            it = seq[:, :, None]
            jb = jt[:, None, :]
            mask = (it < jb) | (it > jb + w) | (jb == -1)
            sim = jnp.einsum('bhwie,bhwje->bhwij', bq, bk2) * QK_SCALE
            sim = jnp.where(mask, -jnp.finfo(sim.dtype).max, sim)
            attn = jax.nn.softmax(sim, -1)
            out = jnp.einsum('bhwij,bhwje->bhwie', attn, bv2)
            return out.reshape(b, h, n, d)

        def attn_layer(x, Wqkv, qs, ksc, Wo):
            b, n, _ = x.shape
            qkv = x @ Wqkv
            q, k, v = jnp.split(qkv, 3, -1)
            sh = lambda t: t.reshape(b, n, HEADS, DIM_HEAD).transpose(0, 2, 1, 3)
            q, k, v = (sh(q), sh(k), sh(v))
            q = l2norm(q) * qs
            k = l2norm(k) * ksc
            freqs, scale = rotary_tables(n)
            cos, sin = (jnp.cos(freqs), jnp.sin(freqs))
            q = q * cos * scale + rotate_half(q) * sin * scale
            inv = 1.0 / scale
            k = k * cos * inv + rotate_half(k) * sin * inv
            out = local_attention(q, k, v)
            out = out.transpose(0, 2, 1, 3).reshape(b, n, INNER)
            return out @ Wo

        def ffn_layer(x, g, bln, W1, b1, W2, b2):
            mu = x.mean(-1, keepdims=True)
            var = ((x - mu) ** 2).mean(-1, keepdims=True)
            xn = (x - mu) / jnp.sqrt(var + 1e-05) * g + bln
            hg = xn @ W1 + b1
            a, gate = jnp.split(hg, 2, -1)
            return a * jax.nn.gelu(gate, approximate=False) @ W2 + b2
        key = jax.random.key(seed)
        ks = jax.random.split(key, 8)
        B, N = (2, 256)
        init = lambda k, shape: jax.random.normal(k, shape, jnp.float32) * 0.02
        return {'x': jax.random.normal(ks[0], (B, N, DIM), jnp.float32), 'Wqkv': init(ks[1], (DEPTH, DIM, 3 * INNER)), 'q_scale': jnp.ones((DEPTH, DIM_HEAD), jnp.float32), 'k_scale': jnp.ones((DEPTH, DIM_HEAD), jnp.float32), 'Wo': init(ks[2], (DEPTH, INNER, DIM)), 'ln_g': jnp.ones((DEPTH, DIM), jnp.float32), 'ln_b': jnp.zeros((DEPTH, DIM), jnp.float32), 'W1': init(ks[3], (DEPTH, DIM, 2 * DIM_INNER)), 'b1': jnp.zeros((DEPTH, 2 * DIM_INNER), jnp.float32), 'W2': init(ks[4], (DEPTH, DIM_INNER, DIM)), 'b2': jnp.zeros((DEPTH, DIM), jnp.float32)}
    _L0_ffn_all = _L0_ffn_setup()
    _L0_ffn_in = {k: v for k, v in _L0_ffn_all.items() if k in ('Wqkv', 'q_scale', 'k_scale', 'Wo', 'ln_g', 'ln_b', 'W1', 'b1', 'W2', 'b2')}
    del _L0_ffn_all
    return {'x': x, 'fside_BxSxS_0': fside_BxSxS_0, 'itok_B_18_1004': itok_B_18_1004, 'L0_cond_Wq': _L0_cond_in['Wq'], 'L0_cond_bq': _L0_cond_in['bq'], 'L0_cond_Wk': _L0_cond_in['Wk'], 'L0_cond_bk': _L0_cond_in['bk'], 'L0_cond_Wv': _L0_cond_in['Wv'], 'L0_cond_bv': _L0_cond_in['bv'], 'L0_cond_Wo': _L0_cond_in['Wo'], 'L0_cond_bo': _L0_cond_in['bo'], 'L0_cond_b_prev': _L0_cond_in['b_prev'], 'L0_cond_b_self': _L0_cond_in['b_self'], 'L0_ffn_Wqkv': _L0_ffn_in['Wqkv'], 'L0_ffn_q_scale': _L0_ffn_in['q_scale'], 'L0_ffn_k_scale': _L0_ffn_in['k_scale'], 'L0_ffn_Wo': _L0_ffn_in['Wo'], 'L0_ffn_ln_g': _L0_ffn_in['ln_g'], 'L0_ffn_ln_b': _L0_ffn_in['ln_b'], 'L0_ffn_W1': _L0_ffn_in['W1'], 'L0_ffn_b1': _L0_ffn_in['b1'], 'L0_ffn_W2': _L0_ffn_in['W2'], 'L0_ffn_b2': _L0_ffn_in['b2']}

def reference(x, fside_BxSxS_0, itok_B_18_1004, L0_cond_Wq, L0_cond_bq, L0_cond_Wk, L0_cond_bk, L0_cond_Wv, L0_cond_bv, L0_cond_Wo, L0_cond_bo, L0_cond_b_prev, L0_cond_b_self, L0_ffn_Wqkv, L0_ffn_q_scale, L0_ffn_k_scale, L0_ffn_Wo, L0_ffn_ln_g, L0_ffn_ln_b, L0_ffn_W1, L0_ffn_b1, L0_ffn_W2, L0_ffn_b2):
    import jax
    import jax.numpy as jnp

    def _L0_cond_ref(seq1, seq2, seq_len1, Wq, bq, Wk, bk, Wv, bv, Wo, bo, b_prev, b_self):
        import jax, jax.numpy as jnp
        import numpy as np
        B, L1, L2, DIN, DOUT, H = (8, 128, 128, 128, 128, 16)
        DH = DOUT // H
        SCALE = 1.0 / np.sqrt(DH).astype(np.float32)
        b, l1, _ = seq1.shape
        l2 = seq2.shape[1]
        query = seq2 + b_self
        key = jnp.concatenate([seq1 + b_prev, seq2 + b_self], 1)
        value = jnp.concatenate([seq1, seq2], 1)
        q = (query @ Wq + bq).reshape(b, l2, H, DH).transpose(0, 2, 1, 3)
        k = (key @ Wk + bk).reshape(b, l1 + l2, H, DH).transpose(0, 2, 1, 3)
        v = (value @ Wv + bv).reshape(b, l1 + l2, H, DH).transpose(0, 2, 1, 3)
        score_prev = jnp.einsum('bhqd,bhkd->bhqk', q, k[:, :, :l1]) * SCALE
        score_self = (q * k[:, :, l1:]).sum(-1, keepdims=True) * SCALE
        mask = jnp.arange(l1)[None, :] < seq_len1[:, None]
        score_prev = jnp.where(mask[:, None, None, :], score_prev, -jnp.inf)
        score = jnp.concatenate([score_prev, score_self], -1)
        weights = jax.nn.softmax(score, axis=-1)
        attn = jnp.einsum('bhqk,bhkd->bhqd', weights[..., :-1], v[:, :, :l1])
        attn = attn + weights[..., -1:] * v[:, :, l1:]
        attn = attn.transpose(0, 2, 1, 3).reshape(b, l2, H * DH)
        return attn @ Wo + bo

    def _L0_ffn_ref(x, Wqkv, q_scale, k_scale, Wo, ln_g, ln_b, W1, b1, W2, b2):
        import jax, jax.numpy as jnp
        import numpy as np
        DIM = 128
        DEPTH = 6
        HEADS = 16
        DIM_HEAD = 64
        WINDOW = 32
        INNER = HEADS * DIM_HEAD
        DIM_INNER = int(DIM * 4 * 2 / 3)
        QK_SCALE = 8.0

        def shift_tokens(t):
            a, s = jnp.split(t, 2, -1)
            s = jnp.pad(s, ((0, 0), (1, 0), (0, 0)))[:, :-1]
            return jnp.concatenate([a, s], -1)

        def l2norm(t):
            return t / jnp.maximum(jnp.linalg.norm(t, axis=-1, keepdims=True), 1e-12)

        def rotate_half(x):
            x1, x2 = jnp.split(x, 2, -1)
            return jnp.concatenate([-x2, x1], -1)

        def rotary_tables(n):
            half = jnp.arange(0, DIM_HEAD, 2, dtype=jnp.float32)
            inv_freq = 1.0 / 10000.0 ** (half / DIM_HEAD)
            t = jnp.arange(n, dtype=jnp.float32)
            freqs = t[:, None] * inv_freq[None, :]
            freqs = jnp.concatenate([freqs, freqs], -1)
            base_scale = (half + 0.4 * DIM_HEAD) / (1.4 * DIM_HEAD)
            power = (t - n // 2) / (WINDOW // 2)
            scale = base_scale[None, :] ** power[:, None]
            scale = jnp.concatenate([scale, scale], -1)
            return (freqs, scale)

        def local_attention(q, k, v):
            b, h, n, d = q.shape
            w = WINDOW
            nw = n // w
            bq = q.reshape(b, h, nw, w, d)
            bk = k.reshape(b, h, nw, w, d)
            bv = v.reshape(b, h, nw, w, d)

            def look(t):
                p = jnp.pad(t, ((0, 0), (0, 0), (1, 0), (0, 0), (0, 0)))
                return jnp.concatenate([p[:, :, :nw], p[:, :, 1:]], axis=3)
            bk2, bv2 = (look(bk), look(bv))
            seq = jnp.arange(n).reshape(nw, w)
            seq_p = jnp.pad(seq, ((1, 0), (0, 0)), constant_values=-1)
            jt = jnp.concatenate([seq_p[:nw], seq_p[1:]], axis=1)
            it = seq[:, :, None]
            jb = jt[:, None, :]
            mask = (it < jb) | (it > jb + w) | (jb == -1)
            sim = jnp.einsum('bhwie,bhwje->bhwij', bq, bk2) * QK_SCALE
            sim = jnp.where(mask, -jnp.finfo(sim.dtype).max, sim)
            attn = jax.nn.softmax(sim, -1)
            out = jnp.einsum('bhwij,bhwje->bhwie', attn, bv2)
            return out.reshape(b, h, n, d)

        def attn_layer(x, Wqkv, qs, ksc, Wo):
            b, n, _ = x.shape
            qkv = x @ Wqkv
            q, k, v = jnp.split(qkv, 3, -1)
            sh = lambda t: t.reshape(b, n, HEADS, DIM_HEAD).transpose(0, 2, 1, 3)
            q, k, v = (sh(q), sh(k), sh(v))
            q = l2norm(q) * qs
            k = l2norm(k) * ksc
            freqs, scale = rotary_tables(n)
            cos, sin = (jnp.cos(freqs), jnp.sin(freqs))
            q = q * cos * scale + rotate_half(q) * sin * scale
            inv = 1.0 / scale
            k = k * cos * inv + rotate_half(k) * sin * inv
            out = local_attention(q, k, v)
            out = out.transpose(0, 2, 1, 3).reshape(b, n, INNER)
            return out @ Wo

        def ffn_layer(x, g, bln, W1, b1, W2, b2):
            mu = x.mean(-1, keepdims=True)
            var = ((x - mu) ** 2).mean(-1, keepdims=True)
            xn = (x - mu) / jnp.sqrt(var + 1e-05) * g + bln
            hg = xn @ W1 + b1
            a, gate = jnp.split(hg, 2, -1)
            return a * jax.nn.gelu(gate, approximate=False) @ W2 + b2
        for i in range(DEPTH):
            x = attn_layer(shift_tokens(x), Wqkv[i], q_scale[i], k_scale[i], Wo[i]) + x
            x = ffn_layer(shift_tokens(x), ln_g[i], ln_b[i], W1[i], b1[i], W2[i], b2[i]) + x
        return x
    x = x + _L0_ffn_ref(_L0_cond_ref(x, fside_BxSxS_0, itok_B_18_1004, L0_cond_Wq, L0_cond_bq, L0_cond_Wk, L0_cond_bk, L0_cond_Wv, L0_cond_bv, L0_cond_Wo, L0_cond_bo, L0_cond_b_prev, L0_cond_b_self), L0_ffn_Wqkv, L0_ffn_q_scale, L0_ffn_k_scale, L0_ffn_Wo, L0_ffn_ln_g, L0_ffn_ln_b, L0_ffn_W1, L0_ffn_b1, L0_ffn_W2, L0_ffn_b2)
    return x

_drawn_inputs = setup_inputs


def setup_inputs(seed=0):
    import zlib

    import numpy as np

    out = dict(_drawn_inputs(seed))
    spreads = {'L0_cond_bq': (0.0, 0.8),
     'L0_cond_bk': (0.0, 0.8),
     'L0_cond_bv': (0.0, 0.327),
     'L0_cond_bo': (0.0, 0.1),
     'L0_ffn_q_scale': (1.0, 0.6),
     'L0_ffn_k_scale': (1.0, 0.6),
     'L0_ffn_ln_g': (1.0, 0.6),
     'L0_ffn_ln_b': (0.0, 0.8),
     'L0_ffn_b1': (0.0, 0.46),
     'L0_ffn_b2': (0.0, 0.1)}
    factors = {'fside_BxSxS_0': 8.0,
     'L0_cond_Wq': 8.0,
     'L0_cond_Wk': 8.0,
     'L0_cond_Wv': 8.0,
     'L0_cond_b_prev': 8.0,
     'L0_cond_b_self': 8.0}
    for name, (base, spread) in spreads.items():
        noise = np.random.default_rng([zlib.crc32(name.encode()), seed]).standard_normal(out[name].shape)
        drawn = base * np.exp(spread * noise) if base else spread * noise
        out[name] = jnp.asarray(drawn.astype(out[name].dtype))
    for name, factor in factors.items():
        out[name] = (out[name] * factor).astype(out[name].dtype)
    return out
```

```python
from contextlib import ExitStack

import concourse.bass as bass
from concourse import mybir

F32 = mybir.dt.float32
BF16 = mybir.dt.bfloat16
I32 = mybir.dt.int32
ALU = mybir.AluOpType
ACT = mybir.ActivationFunctionType
AX = mybir.AxisListType

NEG = -1.0e30
EXP_LN = "natural_log_exp_and_others"


def build(nc, t):
    B, N, D = t["x"].shape
    L = t["Wqkv"].shape[0]
    DH = t["q_scale"].shape[1]
    INNER = t["Wo"].shape[1]
    H = INNER // DH
    HC = 16
    DC = D // HC
    FI = t["W2"].shape[1]
    FCH = [(c, min(128, FI - c)) for c in range(0, FI, 128)]
    GB = 4
    NG = B // GB
    HG = 4
    assert D == 128 and N == 128 and H == 16 and DH == 64 and len(FCH) == 3

    with ExitStack() as ctx:
        def sb(name, shape, dt=F32):
            return ctx.enter_context(nc.sbuf_tensor(name, shape, dt))

        def sem(name):
            return ctx.enter_context(nc.semaphore(name))

        resid = sb("resid", [128, B + 1, 1 + N])
        wqkv = sb("wqkv", [128, 3 * INNER])
        wo = sb("wo", [128, INNER // 128, D])
        w1 = sb("w1", [128, 2 * FI])
        w2 = sb("w2", [128, 3, D])
        par = sb("par", [128, 9])
        scl = sb("scl", [128, 2, DH])
        ident = sb("ident", [128, 128])
        eps = sb("eps", [128, 1])
        identb = sb("identb", [128, 128], BF16)
        maskf = sb("maskf", [128, 128])
        maskb = sb("maskb", [128, HG, 128], BF16)
        rot = sb("rot", [128, 2, 2, DH])
        mean_w = sb("mean_w", [128, 128])
        hsel = sb("hsel", [128, HC])
        iota4 = sb("iota4", [1, HG, 128])
        ones_row = sb("ones_row", [1, 128], BF16)
        xs = sb("xs", [128, 128])
        sq = sb("sq", [128, 4, 512])
        uv = sb("uv", [128, 4, 2, 512])
        tab = sb("tab", [128, 2, 2, DH])
        ss = sb("ss", [128, 32])
        ssm = sb("ssm", [128, 32])
        lnss = sb("lnss", [128, 32])
        rnorm = sb("rnorm", [128, 32])
        qT = sb("qT", [128, 8, 128])
        kT = sb("kT", [128, 8, 128])
        v = sb("v", [128, H, DH + 1])
        nmax = sb("nmax", [128, 4, HG])
        prob = sb("prob", [128, 2, HG, 128])
        probT = sb("probT", [128, 2, HG, 128])
        rl = sb("rl", [128, 4, HG])
        o = sb("o", [128, H, DH])
        oT = sb("oT", [128, 8, 128])
        sx = sb("sx", [128, 2, GB, 128])
        xc = sb("xc", [128, 2, 512])
        xq = sb("xq", [128, 2, 512])
        lv = sb("lv", [128, 2, 512])
        rstd = sb("rstd", [128, 2, 512])
        xg = sb("xg", [128, 2, 512])
        xn = sb("xn", [128, NG, 512])
        gate = sb("gate", [128, 3, 512])
        hid = sb("hid", [128, 3, 512])
        xin = sb("xin", [128, 2, D])
        cw = sb("cw", [128, 4, D])
        cb = sb("cb", [128, 6])
        leni = sb("leni", [1, B], I32)
        lenf = sb("lenf", [1, B])
        mrow = sb("mrow", [1, HG, 128], BF16)
        sT = sb("sT", [128, 2, 128])
        sbT = sb("sbT", [128, 2, 128])
        cq = sb("cq", [128, 128])
        ck = sb("ck", [128, 2, 128])
        km = sb("km", [128, HC, 128])
        qk_self = sb("qk_self", [128, 128])
        cv = sb("cv", [128, HC, DC + 1])
        cvs = sb("cvs", [128, HC, DC])
        nself = sb("nself", [128, HC])
        cmax = sb("cmax", [128, HC])
        cnm = sb("cnm", [128, HC])
        dself = sb("dself", [128, HC])
        eself = sb("eself", [128, HC])
        cden = sb("cden", [128, HC])
        crd = sb("crd", [128, HC])
        cnum = sb("cnum", [128, HC, DC])
        cnum2 = sb("cnum2", [128, HC, DC])
        att = sb("att", [128, HC, DC])
        attT = sb("attT", [128, 128])
        xall = xn[:, :, :].rearrange("p g (a b) -> p (g a) b", a=GB)

        bank = [ctx.enter_context(nc.psum_tensor(f"bank{i}", [128, 512], F32)) for i in range(8)]
        PJ = bank[0:2]
        TR = bank[2:4]
        SC = bank[4:6]
        PT = bank[6]
        OB = bank[7]

        ld_const = sem("ld_const")
        ld_cond = sem("ld_cond")
        ld_attn = sem("ld_attn")
        ld_ffn = sem("ld_ffn")
        ld_xin = sem("ld_xin")
        const_dve = sem("const_dve")
        tab_done = sem("tab_done")
        xs_done = sem("xs_done")
        proj_done = sem("proj_done")
        sq_done = sem("sq_done")
        rot_done = sem("rot_done")
        ss_done = sem("ss_done")
        ssm_done = sem("ssm_done")
        ln_done = sem("ln_done")
        rnorm_done = sem("rnorm_done")
        add_done = sem("add_done")
        qk_done = sem("qk_done")
        v_done = sem("v_done")
        qkT_psum = sem("qkT_psum")
        qkT_done = sem("qkT_done")
        score_done = sem("score_done")
        max_done = sem("max_done")
        prob_done = sem("prob_done")
        probT_psum = sem("probT_psum")
        probT_done = sem("probT_done")
        av_done = sem("av_done")
        rl_done = sem("rl_done")
        o_done = sem("o_done")
        oT_psum = sem("oT_psum")
        oT_done = sem("oT_done")
        wo_done = sem("wo_done")
        resid_done = sem("resid_done")
        sx_done = sem("sx_done")
        mean_done = sem("mean_done")
        xc_done = sem("xc_done")
        xq_done = sem("xq_done")
        var_done = sem("var_done")
        lv_done = sem("lv_done")
        rstd_done = sem("rstd_done")
        xg_done = sem("xg_done")
        xn_done = sem("xn_done")
        up_done = sem("up_done")
        gate_done = sem("gate_done")
        hid_done = sem("hid_done")
        down_done = sem("down_done")
        ffn_done = sem("ffn_done")
        c_tx = sem("c_tx")
        c_sT = sem("c_sT")
        c_sbT = sem("c_sbT")
        c_qk = sem("c_qk")
        c_vp = sem("c_vp")
        c_qke = sem("c_qke")
        c_ve = sem("c_ve")
        c_km = sem("c_km")
        c_prod = sem("c_prod")
        c_self = sem("c_self")
        c_nself = sem("c_nself")
        c_mrow = sem("c_mrow")
        c_sc = sem("c_sc")
        c_red = sem("c_red")
        c_max = sem("c_max")
        c_prob = sem("c_prob")
        c_ptp = sem("c_ptp")
        c_pt = sem("c_pt")
        c_av = sem("c_av")
        c_ds = sem("c_ds")
        c_es = sem("c_es")
        c_tail = sem("c_tail")
        c_att = sem("c_att")
        c_ta = sem("c_ta")
        c_attT = sem("c_attT")
        c_wo = sem("c_wo")
        c_out = sem("c_out")
        y_load = sem("y_load")
        y_psum = sem("y_psum")
        y_done = sem("y_done")
        y_store = sem("y_store")
        y_copy = sem("y_copy")
        c_red2 = sem("c_red2")

        block = ctx.enter_context(nc.Block())

        def heads(g):
            return [8 * (g // 2) + 2 * k + g % 2 for k in range(HG)]

        @block.sync
        def _(sp):
            for dst, src in ((ident, "c_ident"), (maskf, "c_mask"), (hsel, "c_hsel")):
                sp.dma_start(dst[:, :], t[src]).then_inc(ld_const, 16)
            sp.dma_start(rot[:, :, :, :], t["c_rot"]).then_inc(ld_const, 16)
            sp.dma_start(iota4[:, :, :], t["c_iota"]).then_inc(ld_const, 16)
            sp.dma_start(leni[:, :], t["seq_len"]).then_inc(ld_cond, 16)
            for i, w in enumerate(("cWq", "cWk", "cWv", "cWo")):
                sp.dma_start(cw[:, i, :], t[w]).then_inc(ld_cond, 16)
            for i, w in enumerate(("cbq", "cbk", "cbv", "cbo", "b_prev", "b_self")):
                sp.dma_start(cb[:, i:i + 1], t[w]).then_inc(ld_cond, 16)

            def load_xin(n):
                sp.dma_start(xin[:, 0:1, :], t["x"][bass.ds(n, 1), :, :].rearrange("b t d -> t b d")).then_inc(ld_xin, 16)
                sp.dma_start(xin[:, 1:2, :], t["fside"][bass.ds(n, 1), :, :].rearrange("b t d -> t b d")).then_inc(ld_xin, 16)

            def load_attn(l):
                sp.dma_start(wqkv[:, :].unsqueeze(1), t["Wqkv"][bass.ds(l, 1), :, :].rearrange("l p n -> p l n")).then_inc(ld_attn, 16)
                sp.dma_start(wo[:, :, :], t["Wo"][bass.ds(l, 1), :, :].rearrange("l (c p) n -> p (l c) n", p=128)).then_inc(ld_attn, 16)
                sp.dma_start(scl[:, 0:1, :], t["q_scale"][bass.ds(l, 1), :].unsqueeze(0).to_broadcast([128, 1, DH])).then_inc(ld_attn, 16)
                sp.dma_start(scl[:, 1:2, :], t["k_scale"][bass.ds(l, 1), :].unsqueeze(0).to_broadcast([128, 1, DH])).then_inc(ld_attn, 16)

            def load_ffn(l):
                sp.dma_start(w1[:, :].unsqueeze(1), t["W1"][bass.ds(l, 1), :, :].rearrange("l p n -> p l n")).then_inc(ld_ffn, 16)
                sp.dma_start(w2[:, 0:2, :], t["W2"][bass.ds(l, 1), 0:256, :].rearrange("l (c p) n -> p (l c) n", p=128)).then_inc(ld_ffn, 16)
                sp.dma_start(w2[0:FI - 256, 2:3, :], t["W2"][bass.ds(l, 1), 256:FI, :].rearrange("l p n -> p l n")).then_inc(ld_ffn, 16)
                sp.dma_start(par[:, :].unsqueeze(1), t["par"][bass.ds(l, 1), :, :].rearrange("l p n -> p l n")).then_inc(ld_ffn, 16)

            load_xin(0)
            load_attn(0)
            load_ffn(0)
            with sp.Fori(1, B) as n:
                sp.wait_ge(c_tx, n)
                load_xin(n)
            with sp.Fori(1, L) as l:
                sp.wait_ge(resid_done, l * B)
                load_attn(l)
                sp.wait_ge(ffn_done, l * NG)
                load_ffn(l)
            sp.wait_ge(ffn_done, L * NG)
            sp.dma_start(xall[:, :, :], t["x"].rearrange("b t d -> t b d")).then_inc(y_load, 16)
            with sp.Fori(0, NG) as k:
                sp.wait_ge(y_done, k + 1)
                sp.dma_start(t["out"][bass.ds(k * GB, GB), :, :].rearrange("b t d -> t b d"), xall[:, bass.ds(k * GB, GB), :]).then_inc(y_store, 16)
            sp.wait_ge(y_store, NG * 16)

        @block.tensor
        def _(pe):
            def mm(out, lhsT, rhs, start=True, stop=True, group=True):
                return nc.tensor.matmul(out, lhsT, rhs, start=start, stop=stop, skip_group_check=not group)

            def c_transpose(n, first):
                pe.wait_ge(ld_xin, n * 32 + 32)
                if not first:
                    pe.wait_ge(c_sT, n)
                nc.tensor.transpose(PJ[0][:, 0:128], xin[:, 0, :], ident[:, :])
                nc.tensor.transpose(PJ[0][:, 128:256], xin[:, 1, :], ident[:, :]).then_inc(c_tx, 1)

            def c_project(n, first):
                pe.wait_ge(c_sbT, n + 1)
                if not first:
                    pe.wait_ge(c_qke, n * 2)
                mm(PJ[1][:, 0:128], cw[:, 0, :], sbT[:, 1, :])
                mm(PJ[1][:, 128:384], cw[:, 1, :], sbT[:, :, :].rearrange("p a b -> p (a b)")).then_inc(c_qk, 1)
                if not first:
                    pe.wait_ge(c_ve, n * 2)
                mm(TR[0][:, 0:128], sT[:, 0, :], cw[:, 2, :])
                mm(TR[0][:, 128:256], sT[:, 1, :], cw[:, 2, :]).then_inc(c_vp, 1)

            def c_self_scores(n, first):
                pe.wait_ge(c_prod, n + 1)
                if not first:
                    pe.wait_ge(c_out, n)
                mm(TR[1][:, 0:HC], qk_self[:, :], hsel[:, :]).then_inc(c_self, 1)

            def c_scores(m, g, first):
                if g == 0:
                    pe.wait_ge(c_mrow, m + 1)
                    pe.wait_ge(c_km, m + 1)
                if g >= 2 or not first:
                    pe.wait_ge(c_prob, m * 4 + g - 1)
                mm(SC[g % 2][:, :], ones_row[:, :], mrow[:, :, :].rearrange("p a b -> p (a b)"), stop=True, group=False)
                mm(SC[g % 2][:, :], cq[:, :], km[:, 4 * g:4 * g + 4, :].rearrange("p a b -> p (a b)"), start=False, group=False).then_inc(c_sc, 1)

            def c_probT(m, g, first):
                pe.wait_ge(c_prob, m * 4 + g + 1)
                if g or not first:
                    pe.wait_ge(c_pt, m * 4 + g)
                for k in range(HG):
                    last = nc.tensor.transpose(PT[:, k * 128:(k + 1) * 128], prob[:, g % 2, k, :], ident[:, :])
                last.then_inc(c_ptp, 1)

            def c_av_(m, g, first):
                pe.wait_ge(c_pt, m * 4 + g + 1)
                if g == 0:
                    pe.wait_ge(c_ve, m * 2 + 2)
                    if not first:
                        pe.wait_ge(c_tail, m * 3)
                for k in range(HG):
                    h = HG * g + k
                    last = mm(OB[:, 9 * h:9 * h + 9], probT[:, g % 2, k, :], cv[:, h, :])
                last.then_inc(c_av, 1)

            def c_output(m):
                pe.wait_ge(c_att, m + 1)
                nc.tensor.transpose(TR[1][:, 128:256], att[:, :, :].rearrange("p a b -> p (a b)"), ident[:, :]).then_inc(c_ta, 1)
                pe.wait_ge(c_attT, m + 1)
                mm(TR[1][:, 256:384], cw[:, 3, :], attT[:, :]).then_inc(c_wo, 1)

            def c_iteration(n, m, first):
                if n is not None:
                    c_transpose(n, m is None)
                if m is not None:
                    c_scores(m, 0, first)
                    c_scores(m, 1, first)
                if n is not None:
                    c_project(n, m is None)
                if m is not None:
                    c_probT(m, 0, first)
                    c_scores(m, 2, first)
                    c_probT(m, 1, first)
                    c_av_(m, 0, first)
                    c_scores(m, 3, first)
                    c_av_(m, 1, first)
                    c_probT(m, 2, first)
                    c_av_(m, 2, first)
                    c_probT(m, 3, first)
                    c_av_(m, 3, first)
                    c_output(m)
                if n is not None:
                    c_self_scores(n, m is None)

            pe.wait_ge(ld_const, 80)
            pe.wait_ge(ld_cond, 176)
            pe.wait_ge(const_dve, 9)
            c_iteration(0, None, True)
            c_iteration(1, 0, True)
            with pe.Fori(2, B) as n:
                c_iteration(n, n - 1, False)
            c_iteration(None, B - 1, False)

            def project(it, c, first):
                if c == 0:
                    pe.wait_ge(xs_done, it * 2 + lx)
                if c >= 2:
                    pe.wait_ge(rot_done, it * 4 + c - 1)
                elif not first:
                    pe.wait_ge(v_done, it * 2 - 1 + c)
                mm(PJ[c % 2][:, :], xs[:, :], wqkv[:, 512 * c:512 * c + 512]).then_inc(proj_done, 1)

            def transpose_qk(jt, i, prev_out):
                c = (i % 2) * 2 + i // 2
                pe.wait_ge(qk_done, jt * 4 + i + 1)
                if i >= 2:
                    pe.wait_ge(qkT_done, jt * 4 + i - 1)
                elif i == 0 and prev_out:
                    pe.wait_ge(resid_done, jt - 1)
                for k in range(4):
                    last = nc.tensor.transpose(TR[i % 2][:, k * 128:(k + 1) * 128], uv[:, c, 0, k * 128:(k + 1) * 128], ident[:, :])
                last.then_inc(qkT_psum, 1)

            def scores(jt, g, first):
                pe.wait_ge(qkT_done, jt * 4 + 2 + 2 * (g // 2))
                if g >= 2 or not first:
                    pe.wait_ge(prob_done, jt * 4 + g - 1)
                mm(SC[g % 2][:, :], identb[:, :], maskb[:, :, :].rearrange("p a b -> p (a b)"), stop=True, group=False)
                for k, h in enumerate(heads(g)):
                    r = slice(64 * (h % 2), 64 * (h % 2) + 64)
                    last = mm(SC[g % 2][:, k * 128:(k + 1) * 128], qT[r, h // 2, :], kT[r, h // 2, :],
                              start=False, stop=True, group=False)
                last.then_inc(score_done, 1)

            def transpose_prob(jt, g, first):
                pe.wait_ge(prob_done, jt * 4 + g + 1)
                if g or not first:
                    pe.wait_ge(probT_done, jt * 4 + g)
                for k in range(HG):
                    last = nc.tensor.transpose(PT[:, k * 128:(k + 1) * 128], prob[:, g % 2, k, :], ident[:, :])
                last.then_inc(probT_psum, 1)

            def times_v(jt, g, first):
                pe.wait_ge(probT_done, jt * 4 + g + 1)
                if g == 0:
                    pe.wait_ge(v_done, jt * 2 + 2)
                if g or not first:
                    pe.wait_ge(o_done, jt * 4 + g)
                for k, h in enumerate(heads(g)):
                    last = mm(OB[:, 65 * k:65 * k + 65], probT[:, g % 2, k, :], v[:, h, :])
                last.then_inc(av_done, 1)

            def transpose_o(kt, i, S):
                pe.wait_ge(o_done, kt * 4 + 2 * i + 2)
                if S:
                    pe.wait_ge(qkT_done, kt * 4 + 7 + i)
                elif i == 0:
                    pe.wait_ge(resid_done, kt)
                for k in range(4):
                    c = 4 * i + k
                    last = nc.tensor.transpose(TR[i][:, k * 128:(k + 1) * 128],
                                               o[:, 2 * c:2 * c + 2, :].rearrange("p a b -> p (a b)"), ident[:, :])
                last.then_inc(oT_psum, 1)

            def out_project(kt):
                pe.wait_ge(oT_done, kt * 2 + 2)
                for c in range(8):
                    last = mm(TR[0][:, 0:128], wo[:, c, :], oT[:, c, :], start=c == 0, stop=c == 7)
                last.then_inc(wo_done, 1)

            def attention(it, jt, kt, first, prev_out):
                P, S, O = it is not None, jt is not None, kt is not None
                if S:
                    transpose_qk(jt, 0, prev_out)
                    transpose_qk(jt, 1, prev_out)
                if P:
                    project(it, 0, not S)
                if S:
                    transpose_qk(jt, 2, prev_out)
                    transpose_qk(jt, 3, prev_out)
                    scores(jt, 0, first)
                if O:
                    transpose_o(kt, 0, S)
                    transpose_o(kt, 1, S)
                if P:
                    project(it, 1, not S)
                if S:
                    scores(jt, 1, first)
                    transpose_prob(jt, 0, first)
                if P:
                    project(it, 2, not S)
                if S:
                    times_v(jt, 0, first)
                    scores(jt, 2, first)
                    transpose_prob(jt, 1, first)
                if P:
                    project(it, 3, not S)
                if S:
                    scores(jt, 3, first)
                    times_v(jt, 1, first)
                if P:
                    project(it, 4, not S)
                if S:
                    transpose_prob(jt, 2, first)
                if P:
                    project(it, 5, not S)
                if S:
                    times_v(jt, 2, first)
                    transpose_prob(jt, 3, first)
                if O:
                    out_project(kt)
                if S:
                    times_v(jt, 3, first)

            def norm_pair(kt, first):
                for p in range(2):
                    pe.wait_ge(sx_done, (kt + p) * 2 + 2)
                    if not first:
                        pe.wait_ge(xc_done, kt - 1 + p)
                    mm(PJ[p][:, :], mean_w[:, :], sx[:, p, :, :].rearrange("p a b -> p (a b)")).then_inc(mean_done, 1)
                for p in range(2):
                    pe.wait_ge(xq_done, kt + p + 1)
                    if not first:
                        pe.wait_ge(lv_done, kt - 1 + p)
                    mm(TR[p][:, :], mean_w[:, :], xq[:, p, :]).then_inc(var_done, 1)

            def ffn_group(k, kt, first):
                pe.wait_ge(xn_done, kt + NG if first else kt + 1)
                for j, (c0, w) in enumerate(FCH):
                    if not first:
                        pe.wait_ge(hid_done, kt * 3 - 2 + j)
                    x_in = xn[:, bass.ds(k, 1), :].rearrange("p a b -> p (a b)")
                    mm(bank[2 * j][0:w, :], w1[:, FI + c0:FI + c0 + w], x_in).then_inc(up_done, 1)
                    mm(bank[2 * j + 1][0:w, :], w1[:, c0:c0 + w], x_in).then_inc(up_done, 1)
                if not first:
                    pe.wait_ge(ffn_done, kt)
                for j, (c0, w) in enumerate(FCH):
                    pe.wait_ge(hid_done, kt * 3 + 1 + j)
                    last = mm(bank[6][:, :], w2[0:w, j, :], hid[0:w, j, :], start=j == 0, stop=j == 2)
                last.then_inc(down_done, 1)

            with pe.Fori(0, L) as l:
                lx = pe.snap(l * 2 + 2)
                pe.wait_ge(ld_attn, l * 64 + 64)
                base = l * B
                attention(base, None, None, True, False)
                attention(base + 1, base, None, True, False)
                attention(base + 2, base + 1, base, False, False)
                with pe.Fori(3, B) as n:
                    it = pe.snap(base + n)
                    attention(it, it - 1, it - 2, False, True)
                attention(None, base + (B - 1), base + (B - 2), False, True)
                attention(None, None, base + (B - 1), False, True)
                pe.wait_ge(ld_ffn, l * 64 + 64)
                norm_pair(l * NG, True)
                with pe.Fori(1, NG // 2) as k:
                    norm_pair(l * NG + k * 2, False)
                ffn_group(0, l * NG, True)
                with pe.Fori(1, NG) as k:
                    ffn_group(k, l * NG + k, False)

            def result(k, p, first):
                pe.wait_ge(y_copy, k + 1)
                if not first:
                    pe.wait_ge(y_done, k - 1)
                for i in range(GB):
                    last = nc.tensor.transpose(PJ[p][:, i * 128:(i + 1) * 128], sx[:, p, i, :], ident[:, :])
                last.then_inc(y_psum, 1)

            result(0, 0, True)
            result(1, 1, True)
            with pe.Fori(1, NG // 2) as k:
                result(k * 2, 0, False)
                result(k * 2 + 1, 1, False)

        @block.scalar
        def _(act):
            nc.scalar.preload_act_table_set(EXP_LN)

            def c_values(n, first):
                act.wait_ge(c_vp, n + 1)
                if not first:
                    act.wait_ge(c_av, n * 4)
                    act.wait_ge(c_tail, n * 3)
                nc.scalar.copy(cv[:, :, 0:DC], TR[0][:, 0:128].rearrange("p (a b) -> p a b", a=HC)).then_inc(c_ve, 1)
                nc.scalar.copy(cvs[:, :, :].rearrange("p a b -> p (a b)"), TR[0][:, 128:256]).then_inc(c_ve, 1)

            def c_exp(m, g, first):
                act.wait_ge(c_max, m * 4 + g + 1)
                if g >= 2 or not first:
                    act.wait_ge(c_ptp, m * 4 + g - 1)
                for k in range(HG):
                    h = HG * g + k
                    last = nc.scalar.activation(prob[:, g % 2, k, :], SC[g % 2][:, k * 128:(k + 1) * 128], ACT.Exp,
                                                bias=cnm[:, h:h + 1])
                last.then_inc(c_prob, 1)

            def c_exp_self(m):
                act.wait_ge(c_ds, m + 1)
                nc.scalar.activation(eself[:, :], dself[:, :], ACT.Exp).then_inc(c_es, 1)

            def c_iteration(n, m, first):
                if m is not None:
                    for g in range(4):
                        c_exp(m, g, first)
                    c_exp_self(m)
                if n is not None:
                    c_values(n, m is None)

            c_iteration(0, None, True)
            c_iteration(1, 0, True)
            with act.Fori(2, B) as n:
                c_iteration(n, n - 1, False)
            c_iteration(None, B - 1, False)

            def copy_qkT(jt, i):
                act.wait_ge(qkT_psum, jt * 4 + i + 1)
                dst = (qT, kT)[i % 2]
                nc.scalar.copy(dst[:, 4 * (i // 2):4 * (i // 2) + 4, :].rearrange("p a b -> p (a b)"), TR[i % 2][:, :]).then_inc(qkT_done, 1)

            def square(it, c, first):
                act.wait_ge(proj_done, it * 6 + c + 1)
                if not first:
                    act.wait_ge(ss_done, it * 4 - 3 + c)
                nc.scalar.activation(sq[:, c, :], PJ[c % 2][:, :], ACT.Square).then_inc(sq_done, 1)

            def inverse_norms(it):
                act.wait_ge(ssm_done, it + 1)
                nc.scalar.activation(lnss[:, :], ssm[:, :], ACT.Ln).then_inc(ln_done, 1)
                act.wait_ge(ln_done, it + 1)
                nc.scalar.activation(rnorm[:, :], lnss[:, :], ACT.Exp, scale=-0.5).then_inc(rnorm_done, 1)

            def copy_v(it, c, first):
                act.wait_ge(proj_done, it * 6 + c + 1)
                if not first and c == 4:
                    act.wait_ge(av_done, it * 4)
                nc.scalar.copy(v[:, 8 * (c - 4):8 * (c - 4) + 8, 0:DH],
                               PJ[c % 2][:, :].rearrange("p (a b) -> p a b", a=8)).then_inc(v_done, 1)

            def exps(jt, g, first):
                act.wait_ge(max_done, jt * 4 + g + 1)
                if g >= 2 or not first:
                    act.wait_ge(probT_psum, jt * 4 + g - 1)
                for k in range(HG):
                    last = nc.scalar.activation(prob[:, g % 2, k, :], SC[g % 2][:, k * 128:(k + 1) * 128], ACT.Exp,
                                                bias=nmax[:, g, k:k + 1])
                last.then_inc(prob_done, 1)

            def copy_oT(kt, i, prev_out):
                act.wait_ge(oT_psum, kt * 2 + i + 1)
                if prev_out:
                    act.wait_ge(wo_done, kt)
                nc.scalar.copy(oT[:, 4 * i:4 * i + 4, :].rearrange("p a b -> p (a b)"), TR[i][:, :]).then_inc(oT_done, 1)

            def copy_probT(jt, g, first):
                act.wait_ge(probT_psum, jt * 4 + g + 1)
                if g >= 2 or not first:
                    act.wait_ge(av_done, jt * 4 + g - 1)
                nc.scalar.copy(probT[:, g % 2, :, :].rearrange("p a b -> p (a b)"), PT[:, :]).then_inc(probT_done, 1)

            def attention(it, jt, kt, first, prev_out):
                P, S, O = it is not None, jt is not None, kt is not None
                if S:
                    copy_qkT(jt, 0)
                    copy_qkT(jt, 1)
                if P:
                    square(it, 0, not S)
                if S:
                    copy_qkT(jt, 2)
                    copy_qkT(jt, 3)
                    exps(jt, 0, first)
                if O:
                    copy_oT(kt, 0, prev_out)
                if P:
                    square(it, 1, not S)
                if O:
                    copy_oT(kt, 1, prev_out)
                if S:
                    copy_probT(jt, 0, first)
                    exps(jt, 1, first)
                if P:
                    square(it, 2, not S)
                if S:
                    copy_probT(jt, 1, first)
                if P:
                    square(it, 3, not S)
                if S:
                    exps(jt, 2, first)
                    exps(jt, 3, first)
                    copy_probT(jt, 2, first)
                if P:
                    inverse_norms(it)
                if S:
                    copy_probT(jt, 3, first)
                if P:
                    copy_v(it, 4, not S)
                    copy_v(it, 5, not S)

            def norm_pair(kt):
                for p in range(2):
                    act.wait_ge(xc_done, kt + p + 1)
                    nc.scalar.activation(xq[:, p, :], xc[:, p, :], ACT.Square).then_inc(xq_done, 1)
                for p in range(2):
                    act.wait_ge(var_done, kt + p + 1)
                    nc.scalar.activation(lv[:, p, :], TR[p][:, :], ACT.Ln, bias=eps[:, :]).then_inc(lv_done, 1)
                for p in range(2):
                    act.wait_ge(lv_done, kt + p + 1)
                    nc.scalar.activation(rstd[:, p, :], lv[:, p, :], ACT.Exp, scale=-0.5).then_inc(rstd_done, 1)

            def ffn_group(kt, first):
                for j, (c0, w) in enumerate(FCH):
                    act.wait_ge(up_done, kt * 6 + 2 * j + 1)
                    if not first:
                        act.wait_ge(hid_done, kt * 3 - 2 + j)
                    nc.scalar.activation(gate[0:w, j, :], bank[2 * j][0:w, :], ACT.Gelu,
                                         bias=par[0:w, 3 + j:4 + j]).then_inc(gate_done, 1)

            with act.Fori(0, L) as l:
                nc.scalar.preload_act_table_set(EXP_LN)
                base = l * B
                attention(base, None, None, True, False)
                attention(base + 1, base, None, True, False)
                attention(base + 2, base + 1, base, False, False)
                with act.Fori(3, B) as n:
                    it = act.snap(base + n)
                    attention(it, it - 1, it - 2, False, True)
                attention(None, base + (B - 1), base + (B - 2), False, True)
                attention(None, None, base + (B - 1), False, True)
                with act.Fori(0, NG // 2) as k:
                    norm_pair(l * NG + k * 2)
                nc.scalar.preload_act_table(ACT.Gelu)
                act.wait_ge(ld_ffn, l * 64 + 64)
                ffn_group(l * NG, True)
                with act.Fori(1, NG) as k:
                    ffn_group(l * NG + k, False)

        @block.vector
        def _(dve):
            nc.vector.memset(eps[:, :], 1e-5).then_inc(const_dve, 1)
            nc.vector.memset(resid[:, 0:B, 0:1], 0.0).then_inc(const_dve, 1)
            nc.vector.memset(resid[:, B:B + 1, :], 0.0).then_inc(const_dve, 1)
            nc.vector.memset(v[:, :, DH:DH + 1], 1.0).then_inc(const_dve, 1)
            nc.vector.memset(cv[:, :, DC:DC + 1], 1.0).then_inc(const_dve, 1)
            nc.vector.memset(mean_w[:, :], 1.0 / D).then_inc(const_dve, 1)
            nc.vector.memset(ones_row[:, :], 1.0).then_inc(const_dve, 1)
            dve.wait_ge(ld_const, 80)
            nc.vector.tensor_copy(identb[:, :], ident[:, :]).then_inc(const_dve, 1)
            nc.vector.tensor_copy(maskb[:, :, :], maskf[:, :].unsqueeze(1).to_broadcast([128, HG, 128])).then_inc(const_dve, 1)
            dve.wait_ge(ld_cond, 176)
            nc.vector.tensor_copy(lenf[:, :], leni[:, :]).then_inc(const_dve, 1)
            dve.wait_ge(const_dve, 10)

            def c_front_a(n, first):
                dve.wait_ge(c_tx, n + 1)
                if not first:
                    dve.wait_ge(c_vp, n)
                    dve.wait_ge(c_sbT, n)
                nc.vector.tensor_copy(sT[:, :, :].rearrange("p a b -> p (a b)"), PJ[0][:, 0:256]).then_inc(c_sT, 1)

            def c_front_b(n, first):
                dve.wait_ge(c_qk, n + 1)
                if not first:
                    dve.wait_ge(c_sc, n * 4)
                    dve.wait_ge(c_km, n)
                    dve.wait_ge(c_prod, n)
                nc.vector.tensor_scalar(cq[:, :], PJ[1][:, 0:128], cb[:, 0:1], DC ** -0.5, ALU.add, ALU.mult).then_inc(c_qke, 1)
                nc.vector.tensor_scalar(ck[:, :, :].rearrange("p a b -> p (a b)"), PJ[1][:, 128:384], cb[:, 1:2], None, ALU.add).then_inc(c_qke, 1)
                nc.vector.tensor_scalar(mrow[:, :, :].rearrange("p a b -> p (a b)"), iota4[:, :, :].rearrange("p a b -> p (a b)"),
                                        lenf[:, bass.ds(n, 1)], NEG, ALU.is_ge, ALU.mult).then_inc(c_mrow, 1)

            def c_front_c(n):
                dve.wait_ge(c_self, n + 1)
                nc.vector.tensor_scalar(nself[:, :], TR[1][:, 0:HC], -1.0, None, ALU.mult).then_inc(c_nself, 1)

            def c_group_max(m, g):
                dve.wait_ge(c_sc, m * 4 + g + 1)
                hs = slice(HG * g, HG * g + HG)
                nc.vector.tensor_reduce(cmax[:, hs], SC[g % 2][:, :].rearrange("p (a b) -> p a b", a=HG), AX.X, ALU.max,
                                        negate=True).then_inc(c_red, 1)
                dve.wait_ge(c_red, m * 4 + g + 1)
                dve.wait_ge(c_nself, m + 1)
                nc.vector.tensor_tensor(cnm[:, hs], cmax[:, hs], nself[:, hs], ALU.min).then_inc(c_max, 1)
                if g == 3:
                    dve.wait_ge(c_max, m * 4 + 4)
                    nc.vector.tensor_tensor(dself[:, :], cnm[:, :], nself[:, :], ALU.subtract).then_inc(c_ds, 1)

            def c_copy_probT(m, g, first):
                dve.wait_ge(c_ptp, m * 4 + g + 1)
                if g >= 2 or not first:
                    dve.wait_ge(c_av, m * 4 + g - 1)
                nc.vector.tensor_copy(probT[:, g % 2, :, :].rearrange("p a b -> p (a b)"), PT[:, :]).then_inc(c_pt, 1)

            def c_back(m):
                ov = OB[:, 0:9 * HC].rearrange("p (a b) -> p a b", a=HC)
                dve.wait_ge(c_av, m * 4 + 4)
                dve.wait_ge(c_es, m + 1)
                dve.wait_ge(c_ve, m * 2 + 2)
                nc.vector.tensor_tensor(cden[:, :], ov[:, :, DC], eself[:, :], ALU.add).then_inc(c_tail, 1)
                nc.vector.tensor_tensor(cnum[:, :, :], cvs[:, :, :], eself[:, :].unsqueeze(2).to_broadcast([128, HC, DC]), ALU.mult).then_inc(c_tail, 1)
                dve.wait_ge(c_tail, m * 3 + 2)
                nc.vector.reciprocal(crd[:, :], cden[:, :]).then_inc(c_red2, 1)
                nc.vector.tensor_tensor(cnum2[:, :, :], cnum[:, :, :], ov[:, :, 0:DC], ALU.add).then_inc(c_tail, 1)
                dve.wait_ge(c_tail, m * 3 + 3)
                dve.wait_ge(c_red2, m + 1)
                nc.vector.tensor_tensor(att[:, :, :], cnum2[:, :, :], crd[:, :].unsqueeze(2).to_broadcast([128, HC, DC]), ALU.mult).then_inc(c_att, 1)
                dve.wait_ge(c_ta, m + 1)
                nc.vector.tensor_scalar(attT[:, :], TR[1][:, 128:256], cb[:, 2:3], None, ALU.add).then_inc(c_attT, 1)
                dve.wait_ge(c_wo, m + 1)
                nc.vector.tensor_scalar(resid[:, bass.ds(m, 1), 1:1 + N], TR[1][:, 256:384].unsqueeze(1), cb[:, 3:4], None, ALU.add).then_inc(c_out, 1)

            def c_iteration(n, m, first):
                if n is not None:
                    c_front_a(n, m is None)
                if m is not None:
                    c_group_max(m, 0)
                    c_group_max(m, 1)
                    c_copy_probT(m, 0, first)
                    c_group_max(m, 2)
                    c_copy_probT(m, 1, first)
                    c_group_max(m, 3)
                    c_copy_probT(m, 2, first)
                if n is not None:
                    c_front_b(n, m is None)
                if m is not None:
                    c_copy_probT(m, 3, first)
                    c_back(m)
                if n is not None:
                    c_front_c(n)

            c_iteration(0, None, True)
            c_iteration(1, 0, True)
            with dve.Fori(2, B) as n:
                c_iteration(n, n - 1, False)
            c_iteration(None, B - 1, False)

            def shift_xs(n):
                nc.vector.tensor_copy(xs[0:64, :].unsqueeze(1), resid[0:64, bass.ds(n, 1), 1:1 + N]).then_inc(xs_done, 1)
                nc.vector.tensor_copy(xs[64:128, :].unsqueeze(1), resid[64:128, bass.ds(n, 1), 0:N]).then_inc(xs_done, 1)

            def rotate(it, c, first):
                dve.wait_ge(sq_done, it * 4 + c + 1)
                if not first:
                    dve.wait_ge(qkT_psum, it * 4 - 3 + (0, 2, 1, 3)[c])
                q = PJ[c % 2][:, :].rearrange("p (h d) -> p h d", h=8).unsqueeze(1).to_broadcast([128, 2, 8, DH])
                tb = tab[:, c // 2, :, :].unsqueeze(2).to_broadcast([128, 2, 8, DH])
                nc.vector.tensor_tensor(uv[:, c, :, :].rearrange("p a (h d) -> p a h d", h=8), q, tb, ALU.mult).then_inc(rot_done, 1)

            def sum_squares(it, c, first):
                if c == 0 and not first:
                    dve.wait_ge(ssm_done, it)
                nc.vector.tensor_reduce(ss[:, 8 * c:8 * c + 8], sq[:, c, :].rearrange("p (h d) -> p h d", h=8), AX.X, ALU.add).then_inc(ss_done, 1)
                if c == 3:
                    dve.wait_ge(ss_done, it * 4 + 4)
                    if not first:
                        dve.wait_ge(ln_done, it)
                    nc.vector.tensor_scalar(ssm[:, :], ss[:, :], 1e-24, None, ALU.max).then_inc(ssm_done, 1)

            def group_max(jt, g):
                dve.wait_ge(score_done, jt * 4 + g + 1)
                nc.vector.tensor_reduce(nmax[:, g, :], SC[g % 2][:, :].rearrange("p (a b) -> p a b", a=HG), AX.X, ALU.max,
                                        negate=True).then_inc(max_done, 1)

            def normalise(jt, g, first):
                ov = OB[:, 0:65 * HG].rearrange("p (a b) -> p a b", a=HG)
                dve.wait_ge(av_done, jt * 4 + g + 1)
                nc.vector.reciprocal(rl[:, g, :], ov[:, :, DH]).then_inc(rl_done, 1)
                dve.wait_ge(rl_done, jt * 4 + g + 1)
                if g == 0 and not first:
                    dve.wait_ge(oT_psum, jt * 2)
                h0 = heads(g)[0]
                nc.vector.tensor_tensor(o[:, h0:h0 + 7:2, :], ov[:, :, 0:DH], rl[:, g, :].unsqueeze(2).to_broadcast([128, HG, DH]),
                                        ALU.mult).then_inc(o_done, 1)

            def add_resid(k, kt):
                dve.wait_ge(wo_done, kt + 1)
                r = resid[:, bass.ds(k, 1), 1:1 + N]
                nc.vector.tensor_tensor(r, TR[0][:, 0:128].unsqueeze(1), r, ALU.add).then_inc(resid_done, 1)

            def attention(n, it, jt, k, kt, first, prev_out):
                P, S, O = it is not None, jt is not None, kt is not None
                if P:
                    rotate(it, 0, not S)
                if S:
                    group_max(jt, 0)
                if P:
                    sum_squares(it, 0, not S)
                if S:
                    group_max(jt, 1)
                if P:
                    rotate(it, 1, not S)
                if S:
                    normalise(jt, 0, first)
                    group_max(jt, 2)
                if P:
                    sum_squares(it, 1, not S)
                    rotate(it, 2, not S)
                    rotate(it, 3, not S)
                if S:
                    group_max(jt, 3)
                    normalise(jt, 1, first)
                if P:
                    sum_squares(it, 2, not S)
                    sum_squares(it, 3, not S)
                if S:
                    normalise(jt, 2, first)
                if P:
                    dve.wait_ge(proj_done, it * 6 + 6)
                    shift_xs(n + 1)
                if O:
                    add_resid(k, kt)
                if S:
                    normalise(jt, 3, first)

            def norm_pair(k, kt, first):
                for p in range(2):
                    if not first:
                        dve.wait_ge(xc_done, kt - 1 + p)
                        dve.wait_ge(mean_done, kt - 1 + p)
                    for half, off in ((0, 1), (1, 0)):
                        r = slice(64 * half, 64 * half + 64)
                        nc.vector.tensor_copy(sx[r, p, :, :], resid[r, bass.ds((k + p) * GB, GB), off:off + N]).then_inc(sx_done, 1)
                for p in range(2):
                    dve.wait_ge(mean_done, kt + p + 1)
                    dve.wait_ge(sx_done, (kt + p) * 2 + 2)
                    if not first:
                        dve.wait_ge(xg_done, kt - 1 + p)
                    nc.vector.tensor_tensor(xc[:, p, :], sx[:, p, :, :].rearrange("p a b -> p (a b)"), PJ[p][:, :], ALU.subtract).then_inc(xc_done, 1)
                for p in range(2):
                    dve.wait_ge(rstd_done, kt + p + 1)
                    if not first:
                        dve.wait_ge(xn_done, kt - 1 + p)
                    nc.vector.scalar_tensor_tensor(out=xg[:, p, :], in0=xc[:, p, :], scalar=par[:, 7:8], in1=rstd[:, p, :],
                                                   op0=ALU.mult, op1=ALU.mult).then_inc(xg_done, 1)
                for p in range(2):
                    dve.wait_ge(xg_done, kt + p + 1)
                    nc.vector.tensor_scalar(xn[:, bass.ds(k + p, 1), :], xg[:, p:p + 1, :], par[:, 8:9], None, ALU.add).then_inc(xn_done, 1)

            def ffn_group(k, kt):
                for j, (c0, w) in enumerate(FCH):
                    dve.wait_ge(up_done, kt * 6 + 2 * j + 2)
                    dve.wait_ge(gate_done, kt * 3 + j + 1)
                    nc.vector.scalar_tensor_tensor(out=hid[0:w, j, :], in0=bank[2 * j + 1][0:w, :], scalar=par[0:w, j:j + 1],
                                                   in1=gate[0:w, j, :], op0=ALU.add, op1=ALU.mult).then_inc(hid_done, 1)
                dve.wait_ge(down_done, kt + 1)
                r = resid[:, bass.ds(k * GB, GB), 1:1 + N]
                nc.vector.scalar_tensor_tensor(out=r, in0=bank[6][:, :].rearrange("p (a b) -> p a b", a=GB), scalar=par[:, 6:7],
                                               in1=r, op0=ALU.add, op1=ALU.add).then_inc(ffn_done, 1)

            with dve.Fori(0, L) as l:
                dve.wait_ge(ld_attn, l * 64 + 64)
                for i in range(2):
                    nc.vector.tensor_tensor(tab[:, i, :, :], rot[:, i, :, :], scl[:, i, :].unsqueeze(1).to_broadcast([128, 2, DH]),
                                            ALU.mult).then_inc(tab_done, 1)
                dve.wait_ge(tab_done, l * 2 + 2)
                shift_xs(0)
                base = l * B
                attention(0, base, None, None, None, True, False)
                attention(1, base + 1, base, None, None, True, False)
                attention(2, base + 2, base + 1, 0, base, False, False)
                with dve.Fori(3, B) as n:
                    it = dve.snap(base + n)
                    attention(n, it, it - 1, n - 2, it - 2, False, True)
                attention(None, None, base + (B - 1), B - 2, base + (B - 2), False, True)
                attention(None, None, None, B - 1, base + (B - 1), False, True)
                dve.wait_ge(ld_ffn, l * 64 + 64)
                dve.wait_ge(resid_done, l * B + B)
                norm_pair(0, l * NG, True)
                with dve.Fori(1, NG // 2) as k:
                    norm_pair(k * 2, l * NG + k * 2, False)
                ffn_group(0, l * NG)
                with dve.Fori(1, NG) as k:
                    ffn_group(k, l * NG + k)
                dve.wait_ge(ffn_done, l * NG + NG)

            def result(k, p, first):
                if not first:
                    dve.wait_ge(y_psum, k - 1)
                nc.vector.tensor_copy(sx[:, p, :, :], resid[:, bass.ds(k * GB, GB), 1:1 + N]).then_inc(y_copy, 1)

            def result_sum(k, p):
                dve.wait_ge(y_psum, k + 1)
                y = xall[:, bass.ds(k * GB, GB), :]
                nc.vector.tensor_tensor(y, PJ[p][:, :].rearrange("p (a b) -> p a b", a=GB), y, ALU.add).then_inc(y_done, 1)

            result(0, 0, True)
            result(1, 1, True)
            dve.wait_ge(y_load, 16)
            result_sum(0, 0)
            result_sum(1, 1)
            with dve.Fori(1, NG // 2) as k:
                for p in range(2):
                    result(k * 2 + p, p, False)
                for p in range(2):
                    result_sum(k * 2 + p, p)

        @block.gpsimd
        def _(po):
            po.wait_ge(ld_const, 80)
            po.wait_ge(ld_cond, 176)

            def c_bias(n, first):
                po.wait_ge(c_sT, n + 1)
                if not first:
                    po.wait_ge(c_qk, n)
                nc.gpsimd.tensor_tensor(sbT[:, :, :], sT[:, :, :], cb[:, 4:6].unsqueeze(2).to_broadcast([128, 2, 128]), ALU.add).then_inc(c_sbT, 1)

            def c_keys(n, first):
                po.wait_ge(c_qke, n * 2 + 2)
                if not first:
                    po.wait_ge(c_self, n)
                nc.gpsimd.tensor_tensor(qk_self[:, :], cq[:, :], ck[:, 1, :], ALU.mult).then_inc(c_prod, 1)
                if not first:
                    po.wait_ge(c_sc, n * 4)
                nc.gpsimd.tensor_tensor(km[:, :, :], ck[:, 0, :].unsqueeze(1).to_broadcast([128, HC, 128]),
                                        hsel[:, :].unsqueeze(2).to_broadcast([128, HC, 128]), ALU.mult).then_inc(c_km, 1)

            c_bias(0, True)
            c_keys(0, True)
            with po.Fori(1, B) as n:
                c_bias(n, False)
                c_keys(n, False)

            def finish_qk(it, first):
                for c in range(4):
                    po.wait_ge(rot_done, it * 4 + c + 1)
                    u = uv[:, c, 0, :].rearrange("p (h s d) -> p h s d", h=8, s=2)
                    w = uv[:, c, 1, :].rearrange("p (h s d) -> p h s d", h=8, s=2)
                    nc.gpsimd.tensor_tensor(u, u, w[:, :, ::-1, :], ALU.add).then_inc(add_done, 1)
                po.wait_ge(rnorm_done, it + 1)
                for c in (0, 2, 1, 3):
                    po.wait_ge(add_done, it * 4 + c + 1)
                    u = uv[:, c, 0, :].rearrange("p (h d) -> p h d", h=8)
                    nc.gpsimd.tensor_tensor(u, u, rnorm[:, 8 * c:8 * c + 8].unsqueeze(2).to_broadcast([128, 8, DH]), ALU.mult).then_inc(qk_done, 1)

            with po.Fori(0, L) as l:
                with po.Fori(0, B) as n:
                    finish_qk(l * B + n, False)


def _constants(N, DH, HC, D):
    import numpy as np
    f = np.float32
    i, j = np.arange(N)[:, None], np.arange(N)[None, :]
    mask = np.where((j > i) | (i > j + 32), f(NEG), f(0)).astype(f)
    half = np.arange(0, DH, 2, dtype=f)
    inv_freq = (f(1.0) / f(10000.0) ** (half / f(DH))).astype(f)
    tt = np.arange(N, dtype=f)
    freqs = (tt[:, None] * inv_freq[None, :]).astype(f)
    base = (half + f(0.4 * DH)) / f(1.4 * DH)
    power = (tt - N // 2) / f(16)
    scale = (base[None, :] ** power[:, None]).astype(f)
    cos, sin = np.cos(freqs).astype(f), np.sin(freqs).astype(f)
    two = lambda a, b: np.concatenate([a, b], -1)
    rot = np.zeros((N, 2, 2, DH), f)
    rot[:, 0, 0] = two(cos * scale, cos * scale) * f(8)
    rot[:, 0, 1] = two(sin * scale, -sin * scale) * f(8)
    rot[:, 1, 0] = two(cos / scale, cos / scale)
    rot[:, 1, 1] = two(sin / scale, -sin / scale)
    hsel = (np.arange(D)[:, None] // (D // HC) == np.arange(HC)[None, :]).astype(f)
    iota = np.tile(np.arange(N, dtype=f), 4).reshape(1, 4, N)
    return {"c_ident": np.eye(128, dtype=f), "c_mask": mask, "c_rot": rot, "c_hsel": hsel, "c_iota": iota}


def kernel(**inputs):
    import numpy as np
    import concourse.bacc as _bacc
    from concourse import mybir as _mybir
    from concourse.bass_utils import run_bass_kernel_spmd as _run

    a = {k: np.asarray(w) for k, w in inputs.items()}
    col = lambda w: np.ascontiguousarray(w).reshape(-1, 1)
    arrays = {
        "x": a["x"], "fside": a["fside_BxSxS_0"], "seq_len": a["itok_B_18_1004"].reshape(1, -1),
        "cWq": a["L0_cond_Wq"], "cWk": a["L0_cond_Wk"], "cWv": a["L0_cond_Wv"], "cWo": a["L0_cond_Wo"],
        "cbq": col(a["L0_cond_bq"]), "cbk": col(a["L0_cond_bk"]), "cbv": col(a["L0_cond_bv"]), "cbo": col(a["L0_cond_bo"]),
        "b_prev": col(a["L0_cond_b_prev"]), "b_self": col(a["L0_cond_b_self"]),
        "Wqkv": a["L0_ffn_Wqkv"], "q_scale": a["L0_ffn_q_scale"], "k_scale": a["L0_ffn_k_scale"], "Wo": a["L0_ffn_Wo"],
        "W1": a["L0_ffn_W1"], "W2": a["L0_ffn_W2"],
    }
    b1, b2 = a["L0_ffn_b1"], a["L0_ffn_b2"]
    L, FI = b1.shape[0], b1.shape[1] // 2
    par = np.zeros((L, 128, 9), b1.dtype)
    for half in range(2):
        for j, c in enumerate(range(0, FI, 128)):
            w = min(128, FI - c)
            par[:, :w, 3 * half + j] = b1[:, half * FI + c:half * FI + c + w]
    par[:, :, 6], par[:, :, 7], par[:, :, 8] = b2, a["L0_ffn_ln_g"], a["L0_ffn_ln_b"]
    arrays["par"] = par
    arrays.update(_constants(128, 64, 16, 128))
    arrays = {k: np.ascontiguousarray(w) for k, w in arrays.items()}
    nc = _bacc.Bacc("TRN2", target_bir_lowering=False, num_devices=1)
    t = {k: nc.dram_tensor(f"in_{k}", w.shape, _mybir.dt.from_np(w.dtype), kind="ExternalInput").ap() for k, w in arrays.items()}
    t["out"] = nc.dram_tensor("out", a["x"].shape, _mybir.dt.from_np(a["x"].dtype), kind="ExternalOutput").ap()
    build(nc, t)
    r = _run(nc, [{f"in_{k}": w for k, w in arrays.items()}], core_ids=[0])
    return r.results[0]["out"]
```

```python
from contextlib import ExitStack

import concourse.bass as bass
from concourse import mybir

F32 = mybir.dt.float32
F32R = mybir.dt.float32r
BF16 = mybir.dt.bfloat16
I32 = mybir.dt.int32
ALU = mybir.AluOpType
ACT = mybir.ActivationFunctionType
AX = mybir.AxisListType

NEG = -1.0e30
EXP_LN = "natural_log_exp_and_others"


def build(nc, t):
    B, N, D = t["x"].shape
    L = t["Wqkv"].shape[0]
    DH = t["q_scale"].shape[1]
    INNER = t["Wo"].shape[1]
    H = INNER // DH
    HC = 16
    DC = D // HC
    FI = t["W2"].shape[1]
    FCH = [(c, min(128, FI - c)) for c in range(0, FI, 128)]
    GB = 4
    NG = B // GB
    HG = 4
    assert D == 128 and N == 128 and H == 16 and DH == 64 and len(FCH) == 3

    with ExitStack() as ctx:
        def sb(name, shape, dt=F32):
            return ctx.enter_context(nc.sbuf_tensor(name, shape, dt))

        def sem(name):
            return ctx.enter_context(nc.semaphore(name))

        resid = sb("resid", [128, B, 1 + N])
        wqkv = sb("wqkv", [128, 2, 3 * INNER], F32R)
        wo = sb("wo", [128, INNER // 128, D])
        w1 = sb("w1", [128, 2, 2 * FI], F32R)
        w2 = sb("w2", [128, 2, 3, D], F32R)
        w1_raw = sb("w1_raw", [128, 2 * FI])
        w2_raw = sb("w2_raw", [128, 3, D])
        one = sb("one", [128, 1])
        par = sb("par", [128, 9])
        scl = sb("scl", [128, 2, DH])
        ident = sb("ident", [128, 128])
        eps = sb("eps", [128, 1])
        identb = sb("identb", [128, 128], BF16)
        maskf = sb("maskf", [128, 128])
        maskb = sb("maskb", [128, HG, 128], BF16)
        rot = sb("rot", [128, 2, 2, DH])
        mean_w = sb("mean_w", [128, 128])
        hsel = sb("hsel", [128, HC])
        iota4 = sb("iota4", [1, HG, 128])
        ones_row = sb("ones_row", [1, 128], BF16)
        region = sb("region", [128, 12 * 512])
        uv = region[:, 0:4096].rearrange("p (c a n) -> p c a n", c=4, a=2)
        sq = region[:, 4096:6144].rearrange("p (c n) -> p c n", c=4)
        sx, xc, xq, lv, rstd, xg = (region[:, 1024 * i:1024 * i + 1024].rearrange("p (a n) -> p a n", a=2) for i in range(6))
        wqkv_raw = region[:, 0:3 * INNER]
        km = region[:, 4096:6144].rearrange("p (h n) -> p h n", h=HC)
        xall = region[:, 0:B * D].rearrange("p (b n) -> p b n", b=B)
        xs = sb("xs", [128, 2, 128], F32R)
        tab = sb("tab", [128, 2, 2, DH])
        ss = sb("ss", [128, 32])
        ssm = sb("ssm", [128, 32])
        lnss = sb("lnss", [128, 32])
        rnorm = sb("rnorm", [128, 32])
        qT = sb("qT", [128, 8, 128])
        kT = sb("kT", [128, 8, 128])
        v = sb("v", [128, H, DH + 1])
        nmax = sb("nmax", [128, 4, HG])
        prob = sb("prob", [128, 2, HG, 128])
        probT = sb("probT", [128, 2, HG, 128])
        rl = sb("rl", [128, 4, HG])
        o = sb("o", [128, H, DH])
        oT = sb("oT", [128, 8, 128])
        xn = sb("xn", [128, 2, NG, 512], F32R)
        gate = sb("gate", [128, 3, 512])
        hid_raw = sb("hid_raw", [128, 3, 512])
        hid = sb("hid", [128, 2, 2, 3, 512], F32R)
        xin = sb("xin", [128, 2, D])
        cw = sb("cw", [128, 4, D])
        cb = sb("cb", [128, 6])
        leni = sb("leni", [1, B], I32)
        lenf = sb("lenf", [1, B])
        mrow = sb("mrow", [1, HG, 128], BF16)
        sT = sb("sT", [128, 2, 128])
        sbT = sb("sbT", [128, 2, 128])
        cq = sb("cq", [128, 128])
        ck = sb("ck", [128, 2, 128])
        qk_self = sb("qk_self", [128, 128])
        cv = sb("cv", [128, HC, DC + 1])
        cvs = sb("cvs", [128, HC, DC])
        nself = sb("nself", [128, HC])
        cmax = sb("cmax", [128, HC])
        cnm = sb("cnm", [128, HC])
        dself = sb("dself", [128, HC])
        eself = sb("eself", [128, HC])
        cden = sb("cden", [128, HC])
        crd = sb("crd", [128, HC])
        cnum = sb("cnum", [128, HC, DC])
        cnum2 = sb("cnum2", [128, HC, DC])
        att = sb("att", [128, HC, DC])
        attT = sb("attT", [128, 128])

        bank = [ctx.enter_context(nc.psum_tensor(f"bank{i}", [128, 512], F32)) for i in range(8)]
        PJ = bank[0:2]
        TR = bank[2:4]
        SC = bank[4:6]
        PT = bank[6]
        OB = bank[7]

        ld_const = sem("ld_const")
        ld_cond = sem("ld_cond")
        ld_attn = sem("ld_attn")
        ld_ffn = sem("ld_ffn")
        ld_xin = sem("ld_xin")
        const_dve = sem("const_dve")
        tab_done = sem("tab_done")
        split_attn = sem("split_attn")
        split_ffn = sem("split_ffn")
        split_ffn0 = sem("split_ffn0")
        split_high = sem("split_high")
        xsh_done = sem("xsh_done")
        xnh_done = sem("xnh_done")
        hid_raw_done = sem("hid_raw_done")
        hid_high = sem("hid_high")
        xs_done = sem("xs_done")
        proj_done = sem("proj_done")
        sq_done = sem("sq_done")
        rot_done = sem("rot_done")
        ss_done = sem("ss_done")
        ssm_done = sem("ssm_done")
        ln_done = sem("ln_done")
        rnorm_done = sem("rnorm_done")
        add_done = sem("add_done")
        qk_done = sem("qk_done")
        v_done = sem("v_done")
        qkT_psum = sem("qkT_psum")
        qkT_done = sem("qkT_done")
        score_done = sem("score_done")
        max_done = sem("max_done")
        prob_done = sem("prob_done")
        probT_psum = sem("probT_psum")
        probT_done = sem("probT_done")
        av_done = sem("av_done")
        rl_done = sem("rl_done")
        o_done = sem("o_done")
        oT_psum = sem("oT_psum")
        oT_done = sem("oT_done")
        wo_done = sem("wo_done")
        resid_done = sem("resid_done")
        sx_done = sem("sx_done")
        mean_done = sem("mean_done")
        xc_done = sem("xc_done")
        xq_done = sem("xq_done")
        var_done = sem("var_done")
        lv_done = sem("lv_done")
        rstd_done = sem("rstd_done")
        xg_done = sem("xg_done")
        xn_done = sem("xn_done")
        up_done = sem("up_done")
        gate_done = sem("gate_done")
        hid_done = sem("hid_done")
        down_done = sem("down_done")
        ffn_done = sem("ffn_done")
        c_tx = sem("c_tx")
        c_sT = sem("c_sT")
        c_sbT = sem("c_sbT")
        c_qk = sem("c_qk")
        c_vp = sem("c_vp")
        c_qke = sem("c_qke")
        c_ve = sem("c_ve")
        c_km = sem("c_km")
        c_prod = sem("c_prod")
        c_self = sem("c_self")
        c_nself = sem("c_nself")
        c_mrow = sem("c_mrow")
        c_sc = sem("c_sc")
        c_red = sem("c_red")
        c_max = sem("c_max")
        c_prob = sem("c_prob")
        c_ptp = sem("c_ptp")
        c_pt = sem("c_pt")
        c_av = sem("c_av")
        c_ds = sem("c_ds")
        c_es = sem("c_es")
        c_tail = sem("c_tail")
        c_att = sem("c_att")
        c_ta = sem("c_ta")
        c_attT = sem("c_attT")
        c_wo = sem("c_wo")
        c_out = sem("c_out")
        y_load = sem("y_load")
        y_psum = sem("y_psum")
        y_done = sem("y_done")
        y_store = sem("y_store")
        y_copy = sem("y_copy")
        c_red2 = sem("c_red2")

        block = ctx.enter_context(nc.Block())

        def heads(g):
            return [8 * (g // 2) + 2 * k + g % 2 for k in range(HG)]

        @block.sync
        def _(sp):
            for dst, src in ((ident, "c_ident"), (maskf, "c_mask"), (hsel, "c_hsel")):
                sp.dma_start(dst[:, :], t[src]).then_inc(ld_const, 16)
            sp.dma_start(rot[:, :, :, :], t["c_rot"]).then_inc(ld_const, 16)
            sp.dma_start(iota4[:, :, :], t["c_iota"]).then_inc(ld_const, 16)
            sp.dma_start(leni[:, :], t["seq_len"]).then_inc(ld_cond, 16)
            for i, w in enumerate(("cWq", "cWk", "cWv", "cWo")):
                sp.dma_start(cw[:, i, :], t[w]).then_inc(ld_cond, 16)
            for i, w in enumerate(("cbq", "cbk", "cbv", "cbo", "b_prev", "b_self")):
                sp.dma_start(cb[:, i:i + 1], t[w]).then_inc(ld_cond, 16)

            def load_xin(n):
                sp.dma_start(xin[:, 0:1, :], t["x"][bass.ds(n, 1), :, :].rearrange("b t d -> t b d")).then_inc(ld_xin, 16)
                sp.dma_start(xin[:, 1:2, :], t["fside"][bass.ds(n, 1), :, :].rearrange("b t d -> t b d")).then_inc(ld_xin, 16)

            def load_attn(l):
                sp.dma_start(wqkv_raw.unsqueeze(1), t["Wqkv"][bass.ds(l, 1), :, :].rearrange("l p n -> p l n")).then_inc(ld_attn, 16)
                sp.dma_start(wo[:, :, :], t["Wo"][bass.ds(l, 1), :, :].rearrange("l (c p) n -> p (l c) n", p=128)).then_inc(ld_attn, 16)
                sp.dma_start(scl[:, 0:1, :], t["q_scale"][bass.ds(l, 1), :].unsqueeze(0).to_broadcast([128, 1, DH])).then_inc(ld_attn, 16)
                sp.dma_start(scl[:, 1:2, :], t["k_scale"][bass.ds(l, 1), :].unsqueeze(0).to_broadcast([128, 1, DH])).then_inc(ld_attn, 16)

            def load_ffn(l):
                sp.dma_start(w1_raw[:, :].unsqueeze(1), t["W1"][bass.ds(l, 1), :, :].rearrange("l p n -> p l n")).then_inc(ld_ffn, 16)
                sp.dma_start(w2_raw[:, 0:2, :], t["W2"][bass.ds(l, 1), 0:256, :].rearrange("l (c p) n -> p (l c) n", p=128)).then_inc(ld_ffn, 16)
                sp.dma_start(w2_raw[0:FI - 256, 2:3, :], t["W2"][bass.ds(l, 1), 256:FI, :].rearrange("l p n -> p l n")).then_inc(ld_ffn, 16)
                sp.dma_start(par[:, :].unsqueeze(1), t["par"][bass.ds(l, 1), :, :].rearrange("l p n -> p l n")).then_inc(ld_ffn, 16)

            load_xin(0)
            load_attn(0)
            load_ffn(0)
            with sp.Fori(1, B) as n:
                sp.wait_ge(c_tx, n)
                load_xin(n)
            with sp.Fori(1, L) as l:
                sp.wait_ge(xn_done, l * NG)
                load_attn(l)
                sp.wait_ge(ffn_done, l * NG)
                load_ffn(l)
            sp.wait_ge(ffn_done, L * NG)
            sp.dma_start(xall, t["x"].rearrange("b t d -> t b d")).then_inc(y_load, 16)
            with sp.Fori(0, NG) as k:
                sp.wait_ge(y_done, k + 1)
                sp.dma_start(t["out"][bass.ds(k * GB, GB), :, :].rearrange("b t d -> t b d"), xall[:, bass.ds(k * GB, GB), :]).then_inc(y_store, 16)
            sp.wait_ge(y_store, NG * 16)

        @block.tensor
        def _(pe):
            def mm(out, lhsT, rhs, start=True, stop=True, group=True):
                return nc.tensor.matmul(out, lhsT, rhs, start=start, stop=stop, skip_group_check=not group)

            def mm3(out, lhsT, rhs, start=True, stop=True):
                mm(out, lhsT(0), rhs(0), start, False)
                mm(out, lhsT(0), rhs(1), False, False)
                return mm(out, lhsT(1), rhs(0), False, stop)

            def c_transpose(n, first):
                pe.wait_ge(ld_xin, n * 32 + 32)
                if not first:
                    pe.wait_ge(c_nself, n)
                nc.tensor.transpose(PJ[0][:, 0:128], xin[:, 0, :], ident[:, :])
                nc.tensor.transpose(PJ[0][:, 128:256], xin[:, 1, :], ident[:, :]).then_inc(c_tx, 1)

            def c_project(n, first):
                pe.wait_ge(c_sbT, n + 1)
                if not first:
                    pe.wait_ge(c_qke, n * 2)
                mm(PJ[1][:, 0:128], cw[:, 0, :], sbT[:, 1, :])
                mm(PJ[1][:, 128:384], cw[:, 1, :], sbT[:, :, :].rearrange("p a b -> p (a b)")).then_inc(c_qk, 1)

            def c_project_values(n, first):
                pe.wait_ge(c_sT, n + 1)
                if not first:
                    pe.wait_ge(c_ve, n * 2)
                mm(TR[0][:, 0:128], sT[:, 0, :], cw[:, 2, :])
                mm(TR[0][:, 128:256], sT[:, 1, :], cw[:, 2, :]).then_inc(c_vp, 1)

            def c_self_scores(n):
                pe.wait_ge(c_prod, n + 1)
                mm(PJ[0][:, 256:256 + HC], qk_self[:, :], hsel[:, :]).then_inc(c_self, 1)

            def c_scores(m, g, first):
                if g == 0:
                    pe.wait_ge(c_mrow, m + 1)
                    pe.wait_ge(c_km, m + 1)
                if g >= 2 or not first:
                    pe.wait_ge(c_prob, m * 4 + g - 1)
                mm(SC[g % 2][:, :], ones_row[:, :], mrow[:, :, :].rearrange("p a b -> p (a b)"), stop=True, group=False)
                mm(SC[g % 2][:, :], cq[:, :], km[:, 4 * g:4 * g + 4, :].rearrange("p a b -> p (a b)"), start=False, group=False).then_inc(c_sc, 1)

            def c_probT(m, g, first):
                pe.wait_ge(c_prob, m * 4 + g + 1)
                if g or not first:
                    pe.wait_ge(c_pt, m * 4 + g)
                for k in range(HG):
                    last = nc.tensor.transpose(PT[:, k * 128:(k + 1) * 128], prob[:, g % 2, k, :], ident[:, :])
                last.then_inc(c_ptp, 1)

            def c_av_(m, g, first):
                pe.wait_ge(c_pt, m * 4 + g + 1)
                if g == 0:
                    pe.wait_ge(c_ve, m * 2 + 2)
                    if not first:
                        pe.wait_ge(c_tail, m * 3)
                for k in range(HG):
                    h = HG * g + k
                    last = mm(OB[:, 9 * h:9 * h + 9], probT[:, g % 2, k, :], cv[:, h, :])
                last.then_inc(c_av, 1)

            def c_transpose_out(m, first):
                pe.wait_ge(c_att, m + 1)
                if not first:
                    pe.wait_ge(c_out, m)
                nc.tensor.transpose(TR[1][:, 0:128], att[:, :, :].rearrange("p a b -> p (a b)"), ident[:, :]).then_inc(c_ta, 1)

            def c_output(m):
                pe.wait_ge(c_attT, m + 1)
                mm(TR[1][:, 128:256], cw[:, 3, :], attT[:, :]).then_inc(c_wo, 1)

            def c_iteration(a, b, c, n=None):
                if a is not None:
                    c_transpose(a, n == 0)
                if c is not None:
                    c_probT(c, 3, n == 2)
                    c_av_(c, 2, n == 2)
                if b is not None:
                    c_scores(b, 0, n == 1)
                    c_scores(b, 1, n == 1)
                if c is not None:
                    c_av_(c, 3, n == 2)
                if a is not None:
                    c_project(a, n == 0)
                if b is not None:
                    c_scores(b, 2, n == 1)
                    c_scores(b, 3, n == 1)
                    c_probT(b, 0, n == 1)
                if c is not None:
                    c_transpose_out(c, n == 2)
                if a is not None:
                    c_project_values(a, n == 0)
                if b is not None:
                    c_probT(b, 1, n == 1)
                    c_av_(b, 0, n == 1)
                if c is not None:
                    c_output(c)
                if a is not None:
                    c_self_scores(a)
                if b is not None:
                    c_probT(b, 2, n == 1)
                    c_av_(b, 1, n == 1)

            pe.wait_ge(ld_const, 80)
            pe.wait_ge(ld_cond, 176)
            pe.wait_ge(const_dve, 10)
            c_iteration(0, None, None, 0)
            c_iteration(1, 0, None, 1)
            c_iteration(2, 1, 0, 2)
            with pe.Fori(3, B) as a:
                c_iteration(a, a - 1, a - 2)
            c_iteration(None, B - 1, B - 2)
            c_iteration(None, None, B - 1)

            def project(it, c, first):
                if c == 0:
                    pe.wait_ge(xs_done, it * 2 + 2)
                if c >= 2:
                    pe.wait_ge(rot_done, it * 4 + c - 1)
                elif not first:
                    pe.wait_ge(v_done, it * 2 - 1 + c)
                mm3(PJ[c % 2][:, :], lambda i: xs[:, i, :], lambda i: wqkv[:, i, 512 * c:512 * c + 512]).then_inc(proj_done, 1)

            def transpose_qk(jt, i, n):
                c = (i % 2) * 2 + i // 2
                pe.wait_ge(qk_done, jt * 4 + i + 1)
                if i >= 2:
                    pe.wait_ge(qkT_done, jt * 4 + i - 1)
                elif n == 1:
                    pe.wait_ge(qkT_done, jt * 4 - 1 + i)
                elif n != 0 and i == 0:
                    pe.wait_ge(resid_done, jt - 1)
                elif n != 0:
                    pe.wait_ge(oT_done, jt * 2 - 2)
                for k in range(4):
                    last = nc.tensor.transpose(TR[i % 2][:, k * 128:(k + 1) * 128], uv[:, c, 0, k * 128:(k + 1) * 128], ident[:, :])
                last.then_inc(qkT_psum, 1)

            def scores(jt, g, first):
                pe.wait_ge(qkT_done, jt * 4 + 2 + 2 * (g // 2))
                if g >= 2 or not first:
                    pe.wait_ge(prob_done, jt * 4 + g - 1)
                mm(SC[g % 2][:, :], identb[:, :], maskb[:, :, :].rearrange("p a b -> p (a b)"), stop=True, group=False)
                for k, h in enumerate(heads(g)):
                    r = slice(64 * (h % 2), 64 * (h % 2) + 64)
                    last = mm(SC[g % 2][:, k * 128:(k + 1) * 128], qT[r, h // 2, :], kT[r, h // 2, :],
                              start=False, stop=True, group=False)
                last.then_inc(score_done, 1)

            def transpose_prob(jt, g, first):
                pe.wait_ge(prob_done, jt * 4 + g + 1)
                if g or not first:
                    pe.wait_ge(probT_done, jt * 4 + g)
                for k in range(HG):
                    last = nc.tensor.transpose(PT[:, k * 128:(k + 1) * 128], prob[:, g % 2, k, :], ident[:, :])
                last.then_inc(probT_psum, 1)

            def times_v(jt, g, first):
                pe.wait_ge(probT_done, jt * 4 + g + 1)
                if g % 2 == 0:
                    pe.wait_ge(v_done, jt * 2 + 1 + g // 2)
                if g or not first:
                    pe.wait_ge(o_done, jt * 4 + g)
                for k, h in enumerate(heads(g)):
                    last = mm(OB[:, 65 * k:65 * k + 65], probT[:, g % 2, k, :], v[:, h, :])
                last.then_inc(av_done, 1)

            def transpose_o(kt, i, last_one):
                pe.wait_ge(o_done, kt * 4 + 2 * i + 2)
                if not last_one:
                    pe.wait_ge(qkT_done, kt * 4 + 7 + i)
                elif i == 0:
                    pe.wait_ge(resid_done, kt)
                else:
                    pe.wait_ge(oT_done, kt * 2)
                for k in range(4):
                    c = 4 * i + k
                    last = nc.tensor.transpose(TR[i][:, k * 128:(k + 1) * 128],
                                               o[:, 2 * c:2 * c + 2, :].rearrange("p a b -> p (a b)"), ident[:, :])
                last.then_inc(oT_psum, 1)

            def out_project(kt):
                pe.wait_ge(oT_done, kt * 2 + 2)
                for c in range(8):
                    last = mm(TR[0][:, 0:128], wo[:, c, :], oT[:, c, :], c == 0, c == 7)
                last.then_inc(wo_done, 1)

            def attention(a, b, c, n=None):
                if a is not None:
                    project(a, 0, n == 0)
                if b is not None:
                    scores(b, 0, n == 1)
                    scores(b, 1, n == 1)
                    transpose_qk(b, 3, None)
                if c is not None:
                    transpose_o(c, 0, b is None)
                if a is not None:
                    project(a, 1, n == 0)
                if b is not None:
                    transpose_prob(b, 0, n == 1)
                if a is not None:
                    project(a, 2, n == 0)
                if c is not None:
                    transpose_o(c, 1, b is None)
                if b is not None:
                    scores(b, 2, n == 1)
                    times_v(b, 0, n == 1)
                if a is not None:
                    project(a, 3, n == 0)
                if b is not None:
                    transpose_prob(b, 1, n == 1)
                    scores(b, 3, n == 1)
                if c is not None:
                    out_project(c)
                if b is not None:
                    transpose_prob(b, 2, n == 1)
                    times_v(b, 1, n == 1)
                if a is not None:
                    project(a, 4, n == 0)
                if b is not None:
                    transpose_prob(b, 3, n == 1)
                    times_v(b, 2, n == 1)
                if a is not None:
                    transpose_qk(a, 0, n)
                    project(a, 5, n == 0)
                    transpose_qk(a, 1, n)
                if b is not None:
                    times_v(b, 3, n == 1)
                if a is not None:
                    transpose_qk(a, 2, n)

            def norm_mean(kt, p, first):
                pe.wait_ge(sx_done, kt * 2 + 2)
                if not first:
                    pe.wait_ge(xc_done, kt - 1)
                mm(PJ[p][:, :], mean_w[:, :], sx[:, p, :]).then_inc(mean_done, 1)

            def norm_var(kt, p, first):
                pe.wait_ge(xq_done, kt + 1)
                if not first:
                    pe.wait_ge(lv_done, kt - 1)
                mm(TR[p][:, :], mean_w[:, :], xq[:, p, :]).then_inc(var_done, 1)

            def ffn_up(k, kt, first):
                pe.wait_ge(xn_done, kt + NG if first else kt + 1)
                x_in = lambda i: xn[:, i, bass.ds(k, 1), :].rearrange("p a b -> p (a b)")
                for j, (c0, w) in enumerate(FCH):
                    if not first:
                        pe.wait_ge(hid_raw_done, kt * 3 - 2 + j)
                    mm3(bank[2 * j][0:w, :], lambda i: w1[:, i, FI + c0:FI + c0 + w], x_in).then_inc(up_done, 1)
                    mm3(bank[2 * j + 1][0:w, :], lambda i: w1[:, i, c0:c0 + w], x_in).then_inc(up_done, 1)

            def ffn_down(kt, p, first):
                if not first:
                    pe.wait_ge(ffn_done, kt - 1)
                for j, (c0, w) in enumerate(FCH):
                    pe.wait_ge(hid_done, kt * 3 + 1 + j)
                    last = mm3(bank[6 + p][:, :], lambda i: w2[0:w, i, j, :], lambda i: hid[0:w, p, i, j, :], j == 0, j == 2)
                last.then_inc(down_done, 1)

            with pe.Fori(0, L) as l:
                pe.wait_ge(split_attn, l + 1)
                base = l * B
                attention(base, None, None, 0)
                attention(base + 1, base, None, 1)
                attention(base + 2, base + 1, base, 2)
                with pe.Fori(3, B) as n:
                    a = pe.snap(base + n)
                    attention(a, a - 1, a - 2)
                attention(None, base + (B - 1), base + (B - 2))
                attention(None, None, base + (B - 1))
                k0 = l * NG
                norm_mean(k0, 0, True)
                norm_mean(k0 + 1, 1, True)
                norm_var(k0, 0, True)
                norm_mean(k0 + 2, 0, False)
                norm_var(k0 + 1, 1, True)
                with pe.Fori(1, NG // 2 - 1) as j:
                    norm_mean(k0 + j * 2 + 1, 1, False)
                    norm_var(k0 + j * 2, 0, False)
                    norm_mean(k0 + j * 2 + 2, 0, False)
                    norm_var(k0 + j * 2 + 1, 1, False)
                norm_mean(k0 + (NG - 1), 1, False)
                norm_var(k0 + (NG - 2), 0, False)
                norm_var(k0 + (NG - 1), 1, False)
                pe.wait_ge(split_ffn, l * 2 + 2)
                ffn_up(0, k0, True)
                ffn_up(1, k0 + 1, False)
                ffn_down(k0, 0, True)
                ffn_up(2, k0 + 2, False)
                ffn_down(k0 + 1, 1, True)
                with pe.Fori(1, NG // 2 - 1) as j:
                    for p in range(2):
                        k = pe.snap(j * 2 + p)
                        ffn_up(k + 1, k0 + k + 1, False)
                        ffn_down(k0 + k, p, False)
                ffn_up(NG - 1, k0 + (NG - 1), False)
                ffn_down(k0 + (NG - 2), 0, False)
                ffn_down(k0 + (NG - 1), 1, False)

            def result(k, p, first):
                pe.wait_ge(y_copy, k + 1)
                if not first:
                    pe.wait_ge(y_done, k - 1)
                for i in range(GB):
                    last = nc.tensor.transpose(PJ[p][:, i * 128:(i + 1) * 128], gate[:, p, 128 * i:128 * i + 128], ident[:, :])
                last.then_inc(y_psum, 1)

            result(0, 0, True)
            result(1, 1, True)
            with pe.Fori(1, NG // 2) as k:
                result(k * 2, 0, False)
                result(k * 2 + 1, 1, False)

        @block.scalar
        def _(act):
            nc.scalar.preload_act_table_set(EXP_LN)

            def c_values(n, first):
                act.wait_ge(c_vp, n + 1)
                if not first:
                    act.wait_ge(c_av, n * 4)
                    act.wait_ge(c_tail, n * 3)
                nc.scalar.copy(cv[:, :, 0:DC], TR[0][:, 0:128].rearrange("p (a b) -> p a b", a=HC)).then_inc(c_ve, 1)
                nc.scalar.copy(cvs[:, :, :].rearrange("p a b -> p (a b)"), TR[0][:, 128:256]).then_inc(c_ve, 1)

            def c_exp(m, g, first):
                act.wait_ge(c_max, m * 4 + g + 1)
                if g >= 2 or not first:
                    act.wait_ge(c_ptp, m * 4 + g - 1)
                for k in range(HG):
                    h = HG * g + k
                    last = nc.scalar.activation(prob[:, g % 2, k, :], SC[g % 2][:, k * 128:(k + 1) * 128], ACT.Exp,
                                                bias=cnm[:, h:h + 1])
                last.then_inc(c_prob, 1)

            def c_exp_self(m):
                act.wait_ge(c_ds, m + 1)
                nc.scalar.activation(eself[:, :], dself[:, :], ACT.Exp).then_inc(c_es, 1)

            def c_copy_probT(m, g, first):
                act.wait_ge(c_ptp, m * 4 + g + 1)
                if g >= 2 or not first:
                    act.wait_ge(c_av, m * 4 + g - 1)
                nc.scalar.copy(probT[:, g % 2, :, :].rearrange("p a b -> p (a b)"), PT[:, :]).then_inc(c_pt, 1)

            def c_iteration(m, first):
                c_exp(m, 0, first)
                c_exp(m, 1, first)
                c_values(m, first)
                c_copy_probT(m, 0, first)
                c_exp(m, 2, first)
                c_copy_probT(m, 1, first)
                c_exp(m, 3, first)
                c_copy_probT(m, 2, first)
                c_copy_probT(m, 3, first)
                c_exp_self(m)

            c_iteration(0, True)
            with act.Fori(1, B) as m:
                c_iteration(m, False)

            def copy_qkT(jt, i):
                act.wait_ge(qkT_psum, jt * 4 + i + 1)
                dst = (qT, kT)[i % 2]
                nc.scalar.copy(dst[:, 4 * (i // 2):4 * (i // 2) + 4, :].rearrange("p a b -> p (a b)"), TR[i % 2][:, :]).then_inc(qkT_done, 1)

            def square(it, c, first):
                act.wait_ge(proj_done, it * 6 + c + 1)
                if not first:
                    act.wait_ge(ss_done, it * 4 - 3 + c)
                nc.scalar.activation(sq[:, c, :], PJ[c % 2][:, :], ACT.Square).then_inc(sq_done, 1)

            def inverse_norms(it):
                act.wait_ge(ssm_done, it + 1)
                nc.scalar.activation(lnss[:, :], ssm[:, :], ACT.Ln).then_inc(ln_done, 1)
                act.wait_ge(ln_done, it + 1)
                nc.scalar.activation(rnorm[:, :], lnss[:, :], ACT.Exp, scale=-0.5).then_inc(rnorm_done, 1)

            def copy_v(it, c, first):
                act.wait_ge(proj_done, it * 6 + c + 1)
                if not first:
                    act.wait_ge(av_done, it * 4 - 10 + 2 * c)
                nc.scalar.copy(v[:, 8 * (c - 4):8 * (c - 4) + 8, 0:DH],
                               PJ[c % 2][:, :].rearrange("p (a b) -> p a b", a=8)).then_inc(v_done, 1)

            def exps(jt, g, first):
                act.wait_ge(max_done, jt * 4 + g + 1)
                if g >= 2 or not first:
                    act.wait_ge(probT_psum, jt * 4 + g - 1)
                for k in range(HG):
                    last = nc.scalar.activation(prob[:, g % 2, k, :], SC[g % 2][:, k * 128:(k + 1) * 128], ACT.Exp,
                                                bias=nmax[:, g, k:k + 1])
                last.then_inc(prob_done, 1)

            def copy_oT(kt, i, first):
                act.wait_ge(oT_psum, kt * 2 + i + 1)
                if not first:
                    act.wait_ge(wo_done, kt)
                nc.scalar.copy(oT[:, 4 * i:4 * i + 4, :].rearrange("p a b -> p (a b)"), TR[i][:, :]).then_inc(oT_done, 1)

            def copy_probT(jt, g, first):
                act.wait_ge(probT_psum, jt * 4 + g + 1)
                if g >= 2 or not first:
                    act.wait_ge(av_done, jt * 4 + g - 1)
                nc.scalar.copy(probT[:, g % 2, :, :].rearrange("p a b -> p (a b)"), PT[:, :]).then_inc(probT_done, 1)

            def attention(a, b, c, n=None):
                if a is not None:
                    square(a, 0, n == 0)
                if b is not None:
                    exps(b, 0, n == 1)
                    copy_qkT(b, 3)
                if a is not None:
                    square(a, 1, n == 0)
                if b is not None:
                    copy_probT(b, 0, n == 1)
                if c is not None:
                    copy_oT(c, 0, n == 2)
                if a is not None:
                    square(a, 2, n == 0)
                if b is not None:
                    exps(b, 1, n == 1)
                if c is not None:
                    copy_oT(c, 1, n == 2)
                if a is not None:
                    square(a, 3, n == 0)
                if b is not None:
                    copy_probT(b, 1, n == 1)
                    exps(b, 2, n == 1)
                    exps(b, 3, n == 1)
                if a is not None:
                    inverse_norms(a)
                if b is not None:
                    copy_probT(b, 2, n == 1)
                if a is not None:
                    copy_v(a, 4, n == 0)
                if b is not None:
                    copy_probT(b, 3, n == 1)
                if a is not None:
                    copy_qkT(a, 0)
                    copy_qkT(a, 1)
                    copy_v(a, 5, n == 0)
                    copy_qkT(a, 2)

            def norm_square(kt, p):
                act.wait_ge(xc_done, kt + 1)
                nc.scalar.activation(xq[:, p, :], xc[:, p, :], ACT.Square).then_inc(xq_done, 1)

            def norm_rstd(kt, p):
                act.wait_ge(var_done, kt + 1)
                nc.scalar.activation(lv[:, p, :], TR[p][:, :], ACT.Ln, bias=eps[:, :]).then_inc(lv_done, 1)
                act.wait_ge(lv_done, kt + 1)
                nc.scalar.activation(rstd[:, p, :], lv[:, p, :], ACT.Exp, scale=-0.5).then_inc(rstd_done, 1)

            def ffn_gate(kt, first):
                for j, (c0, w) in enumerate(FCH):
                    act.wait_ge(up_done, kt * 6 + 2 * j + 1)
                    if not first:
                        act.wait_ge(hid_raw_done, kt * 3 - 2 + j)
                    nc.scalar.activation(gate[0:w, j, :], bank[2 * j][0:w, :], ACT.Gelu,
                                         bias=par[0:w, 3 + j:4 + j]).then_inc(gate_done, 1)

            def ffn_high(kt, p, two_before):
                for j, (c0, w) in enumerate(FCH):
                    act.wait_ge(hid_raw_done, kt * 3 + j + 1)
                    if two_before:
                        act.wait_ge(down_done, kt - 1)
                    nc.scalar.copy(hid[0:w, p, 0, j, :], hid_raw[0:w, j, :]).then_inc(hid_high, 1)

            with act.Fori(0, L) as l:
                nc.scalar.preload_act_table_set(EXP_LN)
                base = l * B
                attention(base, None, None, 0)
                attention(base + 1, base, None, 1)
                attention(base + 2, base + 1, base, 2)
                with act.Fori(3, B) as n:
                    a = act.snap(base + n)
                    attention(a, a - 1, a - 2)
                attention(None, base + (B - 1), base + (B - 2))
                attention(None, None, base + (B - 1))
                k0 = l * NG
                norm_square(k0, 0)
                norm_square(k0 + 1, 1)
                norm_rstd(k0, 0)
                with act.Fori(1, NG // 2) as j:
                    norm_square(k0 + j * 2, 0)
                    norm_rstd(k0 + j * 2 - 1, 1)
                    norm_square(k0 + j * 2 + 1, 1)
                    norm_rstd(k0 + j * 2, 0)
                norm_rstd(k0 + (NG - 1), 1)
                nc.scalar.preload_act_table(ACT.Gelu)
                act.wait_ge(ld_ffn, l * 64 + 64)
                ffn_gate(k0, True)
                ffn_high(k0, 0, False)
                ffn_gate(k0 + 1, False)
                ffn_high(k0 + 1, 1, False)
                with act.Fori(1, NG // 2) as j:
                    for p in range(2):
                        kt = act.snap(k0 + j * 2 + p)
                        ffn_gate(kt, False)
                        ffn_high(kt, p, True)

        @block.vector
        def _(dve):
            nc.vector.memset(one[:, :], 1.0).then_inc(const_dve, 1)
            nc.vector.memset(eps[:, :], 1e-5).then_inc(const_dve, 1)
            nc.vector.memset(resid[:, 0:B, 0:1], 0.0).then_inc(const_dve, 1)
            nc.vector.memset(v[:, :, DH:DH + 1], 1.0).then_inc(const_dve, 1)
            nc.vector.memset(cv[:, :, DC:DC + 1], 1.0).then_inc(const_dve, 1)
            nc.vector.memset(mean_w[:, :], 1.0 / D).then_inc(const_dve, 1)
            nc.vector.memset(ones_row[:, :], 1.0).then_inc(const_dve, 1)
            dve.wait_ge(ld_const, 80)
            nc.vector.tensor_copy(identb[:, :], ident[:, :]).then_inc(const_dve, 1)
            nc.vector.tensor_copy(maskb[:, :, :], maskf[:, :].unsqueeze(1).to_broadcast([128, HG, 128])).then_inc(const_dve, 1)
            dve.wait_ge(ld_cond, 176)
            nc.vector.tensor_copy(lenf[:, :], leni[:, :]).then_inc(const_dve, 1)
            dve.wait_ge(const_dve, 10)

            def c_front_a(n, first):
                dve.wait_ge(c_tx, n + 1)
                if not first:
                    dve.wait_ge(c_vp, n)
                    dve.wait_ge(c_sbT, n)
                nc.vector.tensor_copy(sT[:, :, :].rearrange("p a b -> p (a b)"), PJ[0][:, 0:256]).then_inc(c_sT, 1)

            def c_front_b(n, first):
                dve.wait_ge(c_qk, n + 1)
                if not first:
                    dve.wait_ge(c_sc, n * 4)
                    dve.wait_ge(c_km, n)
                    dve.wait_ge(c_prod, n)
                nc.vector.tensor_scalar(cq[:, :], PJ[1][:, 0:128], cb[:, 0:1], DC ** -0.5, ALU.add, ALU.mult).then_inc(c_qke, 1)
                nc.vector.tensor_scalar(ck[:, :, :].rearrange("p a b -> p (a b)"), PJ[1][:, 128:384], cb[:, 1:2], None, ALU.add).then_inc(c_qke, 1)
                nc.vector.tensor_scalar(mrow[:, :, :].rearrange("p a b -> p (a b)"), iota4[:, :, :].rearrange("p a b -> p (a b)"),
                                        lenf[:, bass.ds(n, 1)], NEG, ALU.is_ge, ALU.mult).then_inc(c_mrow, 1)

            def c_front_c(n, first):
                dve.wait_ge(c_self, n + 1)
                if not first:
                    dve.wait_ge(c_ds, n)
                nc.vector.tensor_scalar(nself[:, :], PJ[0][:, 256:256 + HC], -1.0, None, ALU.mult).then_inc(c_nself, 1)

            def c_group_max(m, g):
                dve.wait_ge(c_sc, m * 4 + g + 1)
                hs = slice(HG * g, HG * g + HG)
                nc.vector.tensor_reduce(cmax[:, hs], SC[g % 2][:, :].rearrange("p (a b) -> p a b", a=HG), AX.X, ALU.max,
                                        negate=True).then_inc(c_red, 1)
                dve.wait_ge(c_red, m * 4 + g + 1)
                dve.wait_ge(c_nself, m + 1)
                nc.vector.tensor_tensor(cnm[:, hs], cmax[:, hs], nself[:, hs], ALU.min).then_inc(c_max, 1)

            def c_self_difference(m):
                dve.wait_ge(c_max, m * 4 + 4)
                nc.vector.tensor_tensor(dself[:, :], cnm[:, :], nself[:, :], ALU.subtract).then_inc(c_ds, 1)

            def c_back(m):
                ov = OB[:, 0:9 * HC].rearrange("p (a b) -> p a b", a=HC)
                dve.wait_ge(c_av, m * 4 + 4)
                dve.wait_ge(c_es, m + 1)
                dve.wait_ge(c_ve, m * 2 + 2)
                nc.vector.tensor_tensor(cden[:, :], ov[:, :, DC], eself[:, :], ALU.add).then_inc(c_tail, 1)
                nc.vector.tensor_tensor(cnum[:, :, :], cvs[:, :, :], eself[:, :].unsqueeze(2).to_broadcast([128, HC, DC]), ALU.mult).then_inc(c_tail, 1)
                dve.wait_ge(c_tail, m * 3 + 2)
                nc.vector.reciprocal(crd[:, :], cden[:, :]).then_inc(c_red2, 1)
                nc.vector.tensor_tensor(cnum2[:, :, :], cnum[:, :, :], ov[:, :, 0:DC], ALU.add).then_inc(c_tail, 1)
                dve.wait_ge(c_tail, m * 3 + 3)
                dve.wait_ge(c_red2, m + 1)
                nc.vector.tensor_tensor(att[:, :, :], cnum2[:, :, :], crd[:, :].unsqueeze(2).to_broadcast([128, HC, DC]), ALU.mult).then_inc(c_att, 1)

            def c_out_bias(m):
                dve.wait_ge(c_ta, m + 1)
                nc.vector.tensor_scalar(attT[:, :], TR[1][:, 0:128], cb[:, 2:3], None, ALU.add).then_inc(c_attT, 1)

            def c_write_resid(m):
                dve.wait_ge(c_wo, m + 1)
                nc.vector.tensor_scalar(resid[:, bass.ds(m, 1), 1:1 + N], TR[1][:, 128:256].unsqueeze(1), cb[:, 3:4], None, ALU.add).then_inc(c_out, 1)

            def c_iteration(a, b, c, n=None):
                if a is not None:
                    c_front_a(a, n == 0)
                if b is not None:
                    c_group_max(b, 0)
                    c_group_max(b, 1)
                if c is not None:
                    c_back(c)
                if b is not None:
                    c_group_max(b, 2)
                if a is not None:
                    c_front_b(a, n == 0)
                if c is not None:
                    c_out_bias(c)
                if b is not None:
                    c_group_max(b, 3)
                if c is not None:
                    c_write_resid(c)
                if b is not None:
                    c_self_difference(b)
                if a is not None:
                    c_front_c(a, n == 0)

            c_iteration(0, None, None, 0)
            c_iteration(1, 0, None, 1)
            c_iteration(2, 1, 0, 2)
            with dve.Fori(3, B) as a:
                c_iteration(a, a - 1, a - 2)
            c_iteration(None, B - 1, B - 2)
            c_iteration(None, None, B - 1)

            def shift_xs(place, it, first):
                if not first:
                    dve.wait_ge(proj_done, it * 6)
                for half, off in ((0, 1), (1, 0)):
                    r = slice(64 * half, 64 * half + 64)
                    nc.vector.tensor_copy(xs[r, 0:1, :], resid[r, bass.ds(place, 1), off:off + N]).then_inc(xsh_done, 1)
                for half, off in ((0, 1), (1, 0)):
                    r = slice(64 * half, 64 * half + 64)
                    dve.wait_ge(xsh_done, it * 2 + half + 1)
                    nc.vector.tensor_tensor(xs[r, 1:2, :], resid[r, bass.ds(place, 1), off:off + N], xs[r, 0:1, :], ALU.subtract).then_inc(xs_done, 1)

            def rotate(it, c, first):
                dve.wait_ge(sq_done, it * 4 + c + 1)
                if not first:
                    dve.wait_ge(qkT_psum, it * 4 - 3 + (0, 2, 1, 3)[c])
                q = PJ[c % 2][:, :].rearrange("p (h d) -> p h d", h=8).unsqueeze(1).to_broadcast([128, 2, 8, DH])
                tb = tab[:, c // 2, :, :].unsqueeze(2).to_broadcast([128, 2, 8, DH])
                nc.vector.tensor_tensor(uv[:, c, :, :].rearrange("p a (h d) -> p a h d", h=8), q, tb, ALU.mult).then_inc(rot_done, 1)

            def sum_squares(it, c, first):
                dve.wait_ge(sq_done, it * 4 + c + 1)
                if c == 0 and not first:
                    dve.wait_ge(ssm_done, it)
                nc.vector.tensor_reduce(ss[:, 8 * c:8 * c + 8], sq[:, c, :].rearrange("p (h d) -> p h d", h=8), AX.X, ALU.add).then_inc(ss_done, 1)
                if c == 3:
                    dve.wait_ge(ss_done, it * 4 + 4)
                    if not first:
                        dve.wait_ge(ln_done, it)
                    nc.vector.tensor_scalar(ssm[:, :], ss[:, :], 1e-24, None, ALU.max).then_inc(ssm_done, 1)

            def group_max(jt, g):
                dve.wait_ge(score_done, jt * 4 + g + 1)
                nc.vector.tensor_reduce(nmax[:, g, :], SC[g % 2][:, :].rearrange("p (a b) -> p a b", a=HG), AX.X, ALU.max,
                                        negate=True).then_inc(max_done, 1)

            def normalise(jt, g, first):
                ov = OB[:, 0:65 * HG].rearrange("p (a b) -> p a b", a=HG)
                dve.wait_ge(av_done, jt * 4 + g + 1)
                nc.vector.reciprocal(rl[:, g, :], ov[:, :, DH]).then_inc(rl_done, 1)
                dve.wait_ge(rl_done, jt * 4 + g + 1)
                if g % 2 == 0 and not first:
                    dve.wait_ge(oT_psum, jt * 2 - 1 + g // 2)
                h0 = heads(g)[0]
                nc.vector.tensor_tensor(o[:, h0:h0 + 7:2, :], ov[:, :, 0:DH], rl[:, g, :].unsqueeze(2).to_broadcast([128, HG, DH]),
                                        ALU.mult).then_inc(o_done, 1)

            def add_resid(k, kt):
                dve.wait_ge(wo_done, kt + 1)
                r = resid[:, bass.ds(k, 1), 1:1 + N]
                nc.vector.tensor_tensor(r, TR[0][:, 0:128].unsqueeze(1), r, ALU.add).then_inc(resid_done, 1)

            def attention(place, a, b, c, n=None):
                if a is not None:
                    shift_xs(place, a, n == 0)
                if c is not None:
                    normalise(c, 3, n == 2)
                if b is not None:
                    group_max(b, 0)
                if a is not None:
                    rotate(a, 0, n == 0)
                    sum_squares(a, 0, n == 0)
                if b is not None:
                    group_max(b, 1)
                if a is not None:
                    sum_squares(a, 1, n == 0)
                    rotate(a, 1, n == 0)
                    rotate(a, 2, n == 0)
                if b is not None:
                    group_max(b, 2)
                if a is not None:
                    sum_squares(a, 2, n == 0)
                if b is not None:
                    normalise(b, 0, n == 1)
                    group_max(b, 3)
                if a is not None:
                    sum_squares(a, 3, n == 0)
                if c is not None:
                    add_resid(place - 2, c)
                if b is not None:
                    normalise(b, 1, n == 1)
                if a is not None:
                    rotate(a, 3, n == 0)
                if b is not None:
                    normalise(b, 2, n == 1)

            def norm_center(k, kt, p, first):
                if not first:
                    dve.wait_ge(xc_done, kt - 1)
                for half, off in ((0, 1), (1, 0)):
                    r = slice(64 * half, 64 * half + 64)
                    nc.vector.tensor_copy(sx[r, p, :].rearrange("p (a b) -> p a b", a=GB), resid[r, bass.ds(k * GB, GB), off:off + N]).then_inc(sx_done, 1)

            def norm_subtract(kt, p, first=False):
                dve.wait_ge(mean_done, kt + 1)
                if not first:
                    dve.wait_ge(xg_done, kt - 1)
                dve.wait_ge(sx_done, kt * 2 + 2)
                nc.vector.tensor_tensor(xc[:, p, :], sx[:, p, :], PJ[p][:, :], ALU.subtract).then_inc(xc_done, 1)

            def norm_finish(k, kt, p, first=False):
                dve.wait_ge(rstd_done, kt + 1)
                if not first:
                    dve.wait_ge(xn_done, kt - 1)
                nc.vector.scalar_tensor_tensor(out=xg[:, p, :], in0=xc[:, p, :], scalar=par[:, 7:8], in1=rstd[:, p, :],
                                               op0=ALU.mult, op1=ALU.mult).then_inc(xg_done, 1)
                dve.wait_ge(xg_done, kt + 1)
                x = xg[:, p, :].unsqueeze(1)
                nc.vector.tensor_scalar(xn[:, 0, bass.ds(k, 1), :], x, par[:, 8:9], None, ALU.add).then_inc(xnh_done, 1)
                dve.wait_ge(xnh_done, kt + 1)
                nc.vector.scalar_tensor_tensor(out=xn[:, 1, bass.ds(k, 1), :], in0=x, scalar=par[:, 8:9], in1=xn[:, 0, bass.ds(k, 1), :],
                                               op0=ALU.add, op1=ALU.subtract).then_inc(xn_done, 1)

            def ffn_hidden(kt, p, first):
                for j, (c0, w) in enumerate(FCH):
                    dve.wait_ge(up_done, kt * 6 + 2 * j + 2)
                    dve.wait_ge(gate_done, kt * 3 + j + 1)
                    if not first:
                        dve.wait_ge(hid_done, kt * 3 - 2 + j)
                    nc.vector.scalar_tensor_tensor(out=hid_raw[0:w, j, :], in0=bank[2 * j + 1][0:w, :], scalar=par[0:w, j:j + 1],
                                                   in1=gate[0:w, j, :], op0=ALU.add, op1=ALU.mult).then_inc(hid_raw_done, 1)
                    if j:
                        ffn_low(kt, p, j - 1)
                ffn_low(kt, p, 2)

            def ffn_low(kt, p, j):
                w = FCH[j][1]
                dve.wait_ge(hid_high, kt * 3 + j + 1)
                nc.vector.tensor_tensor(hid[0:w, p, 1, j, :], hid_raw[0:w, j, :], hid[0:w, p, 0, j, :], ALU.subtract).then_inc(hid_done, 1)

            def ffn_resid(k, kt, p):
                dve.wait_ge(down_done, kt + 1)
                r = resid[:, bass.ds(k * GB, GB), 1:1 + N]
                nc.vector.scalar_tensor_tensor(out=r, in0=bank[6 + p][:, :].rearrange("p (a b) -> p a b", a=GB), scalar=par[:, 6:7],
                                               in1=r, op0=ALU.add, op1=ALU.add).then_inc(ffn_done, 1)

            with dve.Fori(0, L) as l:
                dve.wait_ge(ld_attn, l * 64 + 64)
                for i in range(2):
                    nc.vector.tensor_tensor(tab[:, i, :, :], rot[:, i, :, :], scl[:, i, :].unsqueeze(1).to_broadcast([128, 2, DH]),
                                            ALU.mult).then_inc(tab_done, 1)
                dve.wait_ge(tab_done, l * 2 + 2)
                base = l * B
                attention(0, base, None, None, 0)
                attention(1, base + 1, base, None, 1)
                attention(2, base + 2, base + 1, base, 2)
                with dve.Fori(3, B) as n:
                    a = dve.snap(base + n)
                    attention(n, a, a - 1, a - 2)
                attention(B, None, base + (B - 1), base + (B - 2))
                attention(B + 1, None, None, base + (B - 1))
                dve.wait_ge(ld_ffn, l * 64 + 64)
                dve.wait_ge(resid_done, l * B + B)
                k0 = l * NG
                norm_center(0, k0, 0, True)
                norm_center(1, k0 + 1, 1, True)
                norm_subtract(k0, 0, True)
                norm_subtract(k0 + 1, 1, True)
                for p in range(2):
                    norm_center(2 + p, k0 + (2 + p), p, False)
                    norm_finish(p, k0 + p, p, True)
                    norm_subtract(k0 + (2 + p), p)
                with dve.Fori(2, NG // 2) as j:
                    for p in range(2):
                        k = dve.snap(j * 2 + p)
                        norm_center(k, k0 + k, p, False)
                        norm_finish(k - 2, k0 + k - 2, p)
                        norm_subtract(k0 + k, p)
                norm_finish(NG - 2, k0 + (NG - 2), 0)
                norm_finish(NG - 1, k0 + (NG - 1), 1)
                ffn_hidden(k0, 0, True)
                ffn_hidden(k0 + 1, 1, False)
                ffn_resid(0, k0, 0)
                with dve.Fori(1, NG // 2) as j:
                    for p in range(2):
                        k = dve.snap(j * 2 + p)
                        ffn_hidden(k0 + k, p, False)
                        ffn_resid(k - 1, k0 + k - 1, 1 - p)
                ffn_resid(NG - 1, k0 + (NG - 1), 1)
                dve.wait_ge(ffn_done, l * NG + NG)

            def result(k, p, first):
                if not first:
                    dve.wait_ge(y_psum, k - 1)
                nc.vector.tensor_copy(gate[:, p, :].rearrange("p (a b) -> p a b", a=GB), resid[:, bass.ds(k * GB, GB), 1:1 + N]).then_inc(y_copy, 1)

            def result_sum(k, p):
                dve.wait_ge(y_psum, k + 1)
                y = xall[:, bass.ds(k * GB, GB), :]
                nc.vector.tensor_tensor(y, PJ[p][:, :].rearrange("p (a b) -> p a b", a=GB), y, ALU.add).then_inc(y_done, 1)

            result(0, 0, True)
            result(1, 1, True)
            dve.wait_ge(y_load, 16)
            result_sum(0, 0)
            result_sum(1, 1)
            with dve.Fori(1, NG // 2) as k:
                for p in range(2):
                    result(k * 2 + p, p, False)
                for p in range(2):
                    result_sum(k * 2 + p, p)

        @block.gpsimd
        def _(po):
            po.wait_ge(ld_const, 80)
            po.wait_ge(ld_cond, 176)
            po.wait_ge(const_dve, 10)

            def c_bias(n, first):
                po.wait_ge(c_sT, n + 1)
                if not first:
                    po.wait_ge(c_qk, n)
                nc.gpsimd.tensor_tensor(sbT[:, :, :], sT[:, :, :], cb[:, 4:6].unsqueeze(2).to_broadcast([128, 2, 128]), ALU.add).then_inc(c_sbT, 1)

            def c_keys(n, first):
                po.wait_ge(c_qke, n * 2 + 2)
                if not first:
                    po.wait_ge(c_self, n)
                nc.gpsimd.tensor_tensor(qk_self[:, :], cq[:, :], ck[:, 1, :], ALU.mult).then_inc(c_prod, 1)
                if not first:
                    po.wait_ge(c_sc, n * 4)
                nc.gpsimd.tensor_tensor(km[:, :, :], ck[:, 0, :].unsqueeze(1).to_broadcast([128, HC, 128]),
                                        hsel[:, :].unsqueeze(2).to_broadcast([128, HC, 128]), ALU.mult).then_inc(c_km, 1)

            c_bias(0, True)
            c_keys(0, True)
            with po.Fori(1, B) as n:
                c_bias(n, False)
                c_keys(n, False)

            def finish_qk(it, first):
                def add(c):
                    po.wait_ge(rot_done, it * 4 + c + 1)
                    u = uv[:, c, 0, :].rearrange("p (h s d) -> p h s d", h=8, s=2)
                    w = uv[:, c, 1, :].rearrange("p (h s d) -> p h s d", h=8, s=2)
                    nc.gpsimd.tensor_tensor(u, u, w[:, :, ::-1, :], ALU.add).then_inc(add_done, 1)

                def times_norm(c):
                    po.wait_ge(add_done, it * 4 + c + 1)
                    u = uv[:, c, 0, :].rearrange("p (h d) -> p h d", h=8)
                    nc.gpsimd.tensor_tensor(u, u, rnorm[:, 8 * c:8 * c + 8].unsqueeze(2).to_broadcast([128, 8, DH]), ALU.mult).then_inc(qk_done, 1)

                for c in (0, 1, 2):
                    add(c)
                po.wait_ge(rnorm_done, it + 1)
                for c in (0, 2, 1):
                    times_norm(c)
                add(3)
                times_norm(3)

            def split(dst, raw, done, before, shape):
                nc.gpsimd.tensor_tensor(dst(0), raw, shape(one[:, :]), ALU.mult).then_inc(split_high, 1)
                po.wait_ge(split_high, before + 1)
                nc.gpsimd.tensor_tensor(dst(1), raw, dst(0), ALU.subtract).then_inc(done, 1)

            def split_attention(l):
                po.wait_ge(ld_attn, l * 64 + 64)
                split(lambda i: wqkv[:, i, :], wqkv_raw, split_attn, l * 4, lambda a: a.to_broadcast([128, 3 * INNER]))

            def split_feedforward(l):
                po.wait_ge(ld_ffn, l * 64 + 64)
                split(lambda i: w1[:, i, :], w1_raw[:, :], split_ffn, l * 4 + 1, lambda a: a.to_broadcast([128, 2 * FI]))
                split(lambda i: w2[:, i, 0:2, :], w2_raw[:, 0:2, :], split_ffn0, l * 4 + 2, lambda a: a.unsqueeze(2).to_broadcast([128, 2, D]))
                split(lambda i: w2[0:FI - 256, i, 2, :], w2_raw[0:FI - 256, 2, :], split_ffn, l * 4 + 3,
                      lambda a: a[0:FI - 256, :].to_broadcast([FI - 256, D]))

            split_attention(0)
            with po.Fori(0, L - 1) as l:
                with po.Fori(0, B) as n:
                    finish_qk(l * B + n, False)
                split_feedforward(l)
                split_attention(l + 1)
            with po.Fori(0, B) as n:
                finish_qk((L - 1) * B + n, False)
            split_feedforward(L - 1)


def _constants(N, DH, HC, D):
    import numpy as np
    f = np.float32
    i, j = np.arange(N)[:, None], np.arange(N)[None, :]
    mask = np.where((j > i) | (i > j + 32), f(NEG), f(0)).astype(f)
    half = np.arange(0, DH, 2, dtype=f)
    inv_freq = (f(1.0) / f(10000.0) ** (half / f(DH))).astype(f)
    tt = np.arange(N, dtype=f)
    freqs = (tt[:, None] * inv_freq[None, :]).astype(f)
    base = (half + f(0.4 * DH)) / f(1.4 * DH)
    power = (tt - N // 2) / f(16)
    scale = (base[None, :] ** power[:, None]).astype(f)
    cos, sin = np.cos(freqs).astype(f), np.sin(freqs).astype(f)
    two = lambda a, b: np.concatenate([a, b], -1)
    rot = np.zeros((N, 2, 2, DH), f)
    rot[:, 0, 0] = two(cos * scale, cos * scale) * f(8)
    rot[:, 0, 1] = two(sin * scale, -sin * scale) * f(8)
    rot[:, 1, 0] = two(cos / scale, cos / scale)
    rot[:, 1, 1] = two(sin / scale, -sin / scale)
    hsel = (np.arange(D)[:, None] // (D // HC) == np.arange(HC)[None, :]).astype(f)
    iota = np.tile(np.arange(N, dtype=f), 4).reshape(1, 4, N)
    return {"c_ident": np.eye(128, dtype=f), "c_mask": mask, "c_rot": rot, "c_hsel": hsel, "c_iota": iota}


def kernel(**inputs):
    import numpy as np
    import concourse.bacc as _bacc
    from concourse import mybir as _mybir
    from concourse.bass_utils import run_bass_kernel_spmd as _run

    a = {k: np.asarray(w) for k, w in inputs.items()}
    col = lambda w: np.ascontiguousarray(w).reshape(-1, 1)
    arrays = {
        "x": a["x"], "fside": a["fside_BxSxS_0"], "seq_len": a["itok_B_18_1004"].reshape(1, -1),
        "cWq": a["L0_cond_Wq"], "cWk": a["L0_cond_Wk"], "cWv": a["L0_cond_Wv"], "cWo": a["L0_cond_Wo"],
        "cbq": col(a["L0_cond_bq"]), "cbk": col(a["L0_cond_bk"]), "cbv": col(a["L0_cond_bv"]), "cbo": col(a["L0_cond_bo"]),
        "b_prev": col(a["L0_cond_b_prev"]), "b_self": col(a["L0_cond_b_self"]),
        "Wqkv": a["L0_ffn_Wqkv"], "q_scale": a["L0_ffn_q_scale"], "k_scale": a["L0_ffn_k_scale"], "Wo": a["L0_ffn_Wo"],
        "W1": a["L0_ffn_W1"], "W2": a["L0_ffn_W2"],
    }
    b1, b2 = a["L0_ffn_b1"], a["L0_ffn_b2"]
    L, FI = b1.shape[0], b1.shape[1] // 2
    par = np.zeros((L, 128, 9), b1.dtype)
    for half in range(2):
        for j, c in enumerate(range(0, FI, 128)):
            w = min(128, FI - c)
            par[:, :w, 3 * half + j] = b1[:, half * FI + c:half * FI + c + w]
    par[:, :, 6], par[:, :, 7], par[:, :, 8] = b2, a["L0_ffn_ln_g"], a["L0_ffn_ln_b"]
    arrays["par"] = par
    arrays.update(_constants(128, 64, 16, 128))
    arrays = {k: np.ascontiguousarray(w) for k, w in arrays.items()}
    nc = _bacc.Bacc("TRN2", target_bir_lowering=False, num_devices=1)
    t = {k: nc.dram_tensor(f"in_{k}", w.shape, _mybir.dt.from_np(w.dtype), kind="ExternalInput").ap() for k, w in arrays.items()}
    t["out"] = nc.dram_tensor("out", a["x"].shape, _mybir.dt.from_np(a["x"].dtype), kind="ExternalOutput").ap()
    build(nc, t)
    r = _run(nc, [{f"in_{k}": w for k, w in arrays.items()}], core_ids=[0])
    return r.results[0]["out"]
```

```python
from contextlib import ExitStack

import concourse.bass as bass
from concourse import mybir

F32 = mybir.dt.float32
F32R = mybir.dt.float32r
BF16 = mybir.dt.bfloat16
I32 = mybir.dt.int32
ALU = mybir.AluOpType
ACT = mybir.ActivationFunctionType
AX = mybir.AxisListType

NEG = -1.0e30
EXP_LN = "natural_log_exp_and_others"


def build(nc, t):
    B, N, D = t["x"].shape
    L = t["Wqkv"].shape[0]
    DH = t["q_scale"].shape[1]
    INNER = t["Wo"].shape[1]
    H = INNER // DH
    HC = 16
    DC = D // HC
    FI = t["W2"].shape[1]
    FCH = [(c, min(128, FI - c)) for c in range(0, FI, 128)]
    GB = 4
    NG = B // GB
    HG = 4
    assert D == 128 and N == 128 and H == 16 and DH == 64 and len(FCH) == 3

    with ExitStack() as ctx:
        def sb(name, shape, dt=F32):
            return ctx.enter_context(nc.sbuf_tensor(name, shape, dt))

        def sem(name):
            return ctx.enter_context(nc.semaphore(name))

        resid = sb("resid", [128, B, 1 + N])
        wqkv = sb("wqkv", [128, 2, 3 * INNER], F32R)
        wo = sb("wo", [128, INNER // 128, D])
        w1 = sb("w1", [128, 2, 2 * FI], F32R)
        w2 = sb("w2", [128, 2, 3, D], F32R)
        w1_raw = sb("w1_raw", [128, 2 * FI])
        w2_raw = sb("w2_raw", [128, 3, D])
        one = sb("one", [128, 1])
        par = sb("par", [128, 9])
        scl = sb("scl", [128, 2, DH])
        ident = sb("ident", [128, 128])
        eps = sb("eps", [128, 1])
        maskf = sb("maskf", [128, 128])
        rot = sb("rot", [128, 2, 2, DH])
        mean_w = sb("mean_w", [128, 128])
        hsel = sb("hsel", [128, HC])
        iota4 = sb("iota4", [1, HG, 128])
        ones_row = sb("ones_row", [1, 128], BF16)
        region = sb("region", [128, 12 * 512])
        uv = region[:, 0:4096].rearrange("p (c a n) -> p c a n", c=4, a=2)
        sq = region[:, 4096:6144].rearrange("p (c n) -> p c n", c=4)
        wqkv_raw = region[:, 0:3 * INNER]
        km = region[:, 4096:6144].rearrange("p (h n) -> p h n", h=HC)
        xall = region[:, 0:B * D].rearrange("p (b n) -> p b n", b=B)
        xs = sb("xs", [128, 2, 128], F32R)
        tab = sb("tab", [128, 2, 2, DH])
        ss = sb("ss", [128, 32])
        ssm = sb("ssm", [128, 32])
        lnss = sb("lnss", [128, 32])
        rnorm = sb("rnorm", [128, 32])
        qT = sb("qT", [128, 8, 128])
        kT = sb("kT", [128, 8, 128])
        v = sb("v", [128, H, DH + 1])
        held = sb("held", [1, 4])
        nmax = sb("nmax", [128, 4, HG])
        masked = sb("masked", [128, 2, HG, 128])
        prob = sb("prob", [128, 2, HG, 128])
        probT = sb("probT", [128, 2, HG, 128])
        rl = sb("rl", [128, 4, HG])
        o = sb("o", [128, H, DH])
        oT = sb("oT", [128, 8, 128])
        sx = sb("sx", [128, N])
        xc = sb("xc", [128, N])
        xq = sb("xq", [128, N])
        lv = sb("lv", [128, N])
        rstd = sb("rstd", [128, N])
        xg = sb("xg", [128, N])
        xn = sb("xn", [128, 2, B, N], F32R)
        gate = sb("gate", [128, 3, 512])
        hid_raw = sb("hid_raw", [128, 3, 512])
        hid = sb("hid", [128, 2, 2, 3, 512], F32R)
        xin = sb("xin", [128, 2, D])
        cw = sb("cw", [128, 4, D])
        cb = sb("cb", [128, 6])
        leni = sb("leni", [1, B], I32)
        lenf = sb("lenf", [1, B])
        mrow = sb("mrow", [1, HG, 128], BF16)
        sT = sb("sT", [128, 2, 128])
        sbT = sb("sbT", [128, 2, 128])
        cq = sb("cq", [128, 128])
        ck = sb("ck", [128, 2, 128])
        qk_self = sb("qk_self", [128, 128])
        cv = sb("cv", [128, HC, DC + 1])
        cvs = sb("cvs", [128, HC, DC])
        nself = sb("nself", [128, HC])
        cmax = sb("cmax", [128, HC])
        cnm = sb("cnm", [128, HC])
        dself = sb("dself", [128, HC])
        eself = sb("eself", [128, HC])
        cden = sb("cden", [128, HC])
        crd = sb("crd", [128, HC])
        cnum = sb("cnum", [128, HC, DC])
        cnum2 = sb("cnum2", [128, HC, DC])
        att = sb("att", [128, HC, DC])
        attT = sb("attT", [128, 128])

        bank = [ctx.enter_context(nc.psum_tensor(f"bank{i}", [128, 512], F32)) for i in range(8)]
        PJ = bank[0:2]
        TR = bank[2:4]
        SC = bank[4:6]
        PT = bank[6]
        OB = bank[7]

        ld_const = sem("ld_const")
        ld_cond = sem("ld_cond")
        ld_attn = sem("ld_attn")
        ld_ffn = sem("ld_ffn")
        ld_xin = sem("ld_xin")
        const_dve = sem("const_dve")
        tab_done = sem("tab_done")
        split_attn = sem("split_attn")
        split_ffn = sem("split_ffn")
        split_ffn0 = sem("split_ffn0")
        split_high = sem("split_high")
        xsh_done = sem("xsh_done")
        xnh_done = sem("xnh_done")
        hid_raw_done = sem("hid_raw_done")
        hid_high = sem("hid_high")
        xs_done = sem("xs_done")
        proj_done = sem("proj_done")
        sq_done = sem("sq_done")
        rot_done = sem("rot_done")
        ss_done = sem("ss_done")
        ssm_done = sem("ssm_done")
        ln_done = sem("ln_done")
        rnorm_done = sem("rnorm_done")
        add_done = sem("add_done")
        qk_done = sem("qk_done")
        v_done = sem("v_done")
        qkT_psum = sem("qkT_psum")
        qkT_done = sem("qkT_done")
        score_done = sem("score_done")
        max_done = sem("max_done")
        prob_done = sem("prob_done")
        probT_psum = sem("probT_psum")
        probT_done = sem("probT_done")
        av_done = sem("av_done")
        rl_done = sem("rl_done")
        o_done = sem("o_done")
        oT_psum = sem("oT_psum")
        oT_done = sem("oT_done")
        wo_done = sem("wo_done")
        resid_done = sem("resid_done")
        sx_done = sem("sx_done")
        mean_done = sem("mean_done")
        xc_done = sem("xc_done")
        xq_done = sem("xq_done")
        var_done = sem("var_done")
        lv_done = sem("lv_done")
        rstd_done = sem("rstd_done")
        xg_done = sem("xg_done")
        xn_done = sem("xn_done")
        up_done = sem("up_done")
        gate_done = sem("gate_done")
        hid_done = sem("hid_done")
        down_done = sem("down_done")
        ffn_done = sem("ffn_done")
        c_tx = sem("c_tx")
        c_sT = sem("c_sT")
        c_sbT = sem("c_sbT")
        c_qk = sem("c_qk")
        c_vp = sem("c_vp")
        c_qke = sem("c_qke")
        c_ve = sem("c_ve")
        c_km = sem("c_km")
        c_prod = sem("c_prod")
        c_self = sem("c_self")
        c_nself = sem("c_nself")
        c_mrow = sem("c_mrow")
        c_sc = sem("c_sc")
        c_red = sem("c_red")
        c_max = sem("c_max")
        c_prob = sem("c_prob")
        c_ptp = sem("c_ptp")
        c_pt = sem("c_pt")
        c_av = sem("c_av")
        c_ds = sem("c_ds")
        c_es = sem("c_es")
        c_tail = sem("c_tail")
        c_att = sem("c_att")
        c_ta = sem("c_ta")
        c_attT = sem("c_attT")
        c_wo = sem("c_wo")
        c_out = sem("c_out")
        y_load = sem("y_load")
        y_psum = sem("y_psum")
        y_done = sem("y_done")
        y_store = sem("y_store")
        y_copy = sem("y_copy")
        c_red2 = sem("c_red2")

        block = ctx.enter_context(nc.Block())

        def heads(g):
            return [8 * (g // 2) + 2 * k + g % 2 for k in range(HG)]

        @block.sync
        def _(sp):
            for dst, src in ((ident, "c_ident"), (maskf, "c_mask"), (hsel, "c_hsel")):
                sp.dma_start(dst[:, :], t[src]).then_inc(ld_const, 16)
            sp.dma_start(rot[:, :, :, :], t["c_rot"]).then_inc(ld_const, 16)
            sp.dma_start(iota4[:, :, :], t["c_iota"]).then_inc(ld_const, 16)
            sp.dma_start(leni[:, :], t["seq_len"]).then_inc(ld_cond, 16)
            for i, w in enumerate(("cWq", "cWk", "cWv", "cWo")):
                sp.dma_start(cw[:, i, :], t[w]).then_inc(ld_cond, 16)
            for i, w in enumerate(("cbq", "cbk", "cbv", "cbo", "b_prev", "b_self")):
                sp.dma_start(cb[:, i:i + 1], t[w]).then_inc(ld_cond, 16)

            def load_xin(n):
                sp.dma_start(xin[:, 0:1, :], t["x"][bass.ds(n, 1), :, :].rearrange("b t d -> t b d")).then_inc(ld_xin, 16)
                sp.dma_start(xin[:, 1:2, :], t["fside"][bass.ds(n, 1), :, :].rearrange("b t d -> t b d")).then_inc(ld_xin, 16)

            def load_attn(l):
                sp.dma_start(wqkv_raw.unsqueeze(1), t["Wqkv"][bass.ds(l, 1), :, :].rearrange("l p n -> p l n")).then_inc(ld_attn, 16)
                sp.dma_start(wo[:, :, :], t["Wo"][bass.ds(l, 1), :, :].rearrange("l (c p) n -> p (l c) n", p=128)).then_inc(ld_attn, 16)
                sp.dma_start(scl[:, 0:1, :], t["q_scale"][bass.ds(l, 1), :].unsqueeze(0).to_broadcast([128, 1, DH])).then_inc(ld_attn, 16)
                sp.dma_start(scl[:, 1:2, :], t["k_scale"][bass.ds(l, 1), :].unsqueeze(0).to_broadcast([128, 1, DH])).then_inc(ld_attn, 16)

            def load_ffn(l):
                sp.dma_start(w1_raw[:, :].unsqueeze(1), t["W1"][bass.ds(l, 1), :, :].rearrange("l p n -> p l n")).then_inc(ld_ffn, 16)
                sp.dma_start(w2_raw[:, 0:2, :], t["W2"][bass.ds(l, 1), 0:256, :].rearrange("l (c p) n -> p (l c) n", p=128)).then_inc(ld_ffn, 16)
                sp.dma_start(w2_raw[0:FI - 256, 2:3, :], t["W2"][bass.ds(l, 1), 256:FI, :].rearrange("l p n -> p l n")).then_inc(ld_ffn, 16)
                sp.dma_start(par[:, :].unsqueeze(1), t["par"][bass.ds(l, 1), :, :].rearrange("l p n -> p l n")).then_inc(ld_ffn, 16)

            load_xin(0)
            load_attn(0)
            load_ffn(0)
            with sp.Fori(1, B) as n:
                sp.wait_ge(c_tx, n)
                load_xin(n)
            with sp.Fori(1, L) as l:
                sp.wait_ge(xn_done, l * B)
                load_attn(l)
                sp.wait_ge(ffn_done, l * NG)
                load_ffn(l)
            sp.wait_ge(ffn_done, L * NG)
            sp.dma_start(xall, t["x"].rearrange("b t d -> t b d")).then_inc(y_load, 16)
            with sp.Fori(0, NG) as k:
                sp.wait_ge(y_done, k + 1)
                sp.dma_start(t["out"][bass.ds(k * GB, GB), :, :].rearrange("b t d -> t b d"), xall[:, bass.ds(k * GB, GB), :]).then_inc(y_store, 16)
            sp.wait_ge(y_store, NG * 16)

        @block.tensor
        def _(pe):
            def mm(out, lhsT, rhs, start=True, stop=True, group=True):
                return nc.tensor.matmul(out, lhsT, rhs, start=start, stop=stop, skip_group_check=not group)

            def mm3(out, lhsT, rhs, start=True, stop=True):
                mm(out, lhsT(0), rhs(0), start, False)
                mm(out, lhsT(0), rhs(1), False, False)
                return mm(out, lhsT(1), rhs(0), False, stop)

            def c_transpose(n, first):
                pe.wait_ge(ld_xin, n * 32 + 32)
                if not first:
                    pe.wait_ge(c_nself, n)
                nc.tensor.transpose(PJ[0][:, 0:128], xin[:, 0, :], ident[:, :])
                nc.tensor.transpose(PJ[0][:, 128:256], xin[:, 1, :], ident[:, :]).then_inc(c_tx, 1)

            def c_project(n, first):
                pe.wait_ge(c_sbT, n + 1)
                if not first:
                    pe.wait_ge(c_qke, n * 2)
                mm(PJ[1][:, 0:128], cw[:, 0, :], sbT[:, 1, :])
                mm(PJ[1][:, 128:384], cw[:, 1, :], sbT[:, :, :].rearrange("p a b -> p (a b)")).then_inc(c_qk, 1)

            def c_project_values(n, first):
                pe.wait_ge(c_sT, n + 1)
                if not first:
                    pe.wait_ge(c_ve, n * 2)
                mm(TR[0][:, 0:128], sT[:, 0, :], cw[:, 2, :])
                mm(TR[0][:, 128:256], sT[:, 1, :], cw[:, 2, :]).then_inc(c_vp, 1)

            def c_self_scores(n):
                pe.wait_ge(c_prod, n + 1)
                mm(PJ[0][:, 256:256 + HC], qk_self[:, :], hsel[:, :]).then_inc(c_self, 1)

            def c_scores(m, g, first):
                if g == 0:
                    pe.wait_ge(c_mrow, m + 1)
                    pe.wait_ge(c_km, m + 1)
                if g >= 2 or not first:
                    pe.wait_ge(c_prob, m * 4 + g - 1)
                mm(SC[g % 2][:, :], ones_row[:, :], mrow[:, :, :].rearrange("p a b -> p (a b)"), stop=True, group=False)
                mm(SC[g % 2][:, :], cq[:, :], km[:, 4 * g:4 * g + 4, :].rearrange("p a b -> p (a b)"), start=False, group=False).then_inc(c_sc, 1)

            def c_probT(m, g, first):
                pe.wait_ge(c_prob, m * 4 + g + 1)
                if g or not first:
                    pe.wait_ge(c_pt, m * 4 + g)
                for k in range(HG):
                    last = nc.tensor.transpose(PT[:, k * 128:(k + 1) * 128], prob[:, g % 2, k, :], ident[:, :])
                last.then_inc(c_ptp, 1)

            def c_times_v(m, g, first):
                pe.wait_ge(c_pt, m * 4 + g + 1)
                if g == 0:
                    pe.wait_ge(c_ve, m * 2 + 2)
                    if not first:
                        pe.wait_ge(c_tail, m * 3)
                for k in range(HG):
                    h = HG * g + k
                    last = mm(OB[:, 9 * h:9 * h + 9], probT[:, g % 2, k, :], cv[:, h, :])
                last.then_inc(c_av, 1)

            def c_transpose_out(m, first):
                pe.wait_ge(c_att, m + 1)
                if not first:
                    pe.wait_ge(c_out, m)
                nc.tensor.transpose(TR[1][:, 0:128], att[:, :, :].rearrange("p a b -> p (a b)"), ident[:, :]).then_inc(c_ta, 1)

            def c_output(m):
                pe.wait_ge(c_attT, m + 1)
                mm(TR[1][:, 128:256], cw[:, 3, :], attT[:, :]).then_inc(c_wo, 1)

            def c_iteration(a, b, c, n=None):
                if a is not None:
                    c_transpose(a, n == 0)
                if c is not None:
                    c_probT(c, 3, n == 2)
                    c_times_v(c, 2, n == 2)
                if b is not None:
                    c_scores(b, 0, n == 1)
                    c_scores(b, 1, n == 1)
                if c is not None:
                    c_times_v(c, 3, n == 2)
                if a is not None:
                    c_project(a, n == 0)
                if b is not None:
                    c_scores(b, 2, n == 1)
                    c_scores(b, 3, n == 1)
                    c_probT(b, 0, n == 1)
                if c is not None:
                    c_transpose_out(c, n == 2)
                if a is not None:
                    c_project_values(a, n == 0)
                if b is not None:
                    c_probT(b, 1, n == 1)
                    c_times_v(b, 0, n == 1)
                if c is not None:
                    c_output(c)
                if a is not None:
                    c_self_scores(a)
                if b is not None:
                    c_probT(b, 2, n == 1)
                    c_times_v(b, 1, n == 1)

            pe.wait_ge(ld_const, 80)
            pe.wait_ge(ld_cond, 176)
            pe.wait_ge(const_dve, 8)
            c_iteration(0, None, None, 0)
            c_iteration(1, 0, None, 1)
            c_iteration(2, 1, 0, 2)
            with pe.Fori(3, B) as a:
                c_iteration(a, a - 1, a - 2)
            c_iteration(None, B - 1, B - 2)
            c_iteration(None, None, B - 1)

            def project(it, c, first):
                if c == 0:
                    pe.wait_ge(xs_done, it * 2 + 2)
                if c >= 2:
                    pe.wait_ge(rot_done, it * 4 + c - 1)
                elif not first:
                    pe.wait_ge(v_done, it * 2 - 1 + c)
                mm3(PJ[c % 2][:, :], lambda i: xs[:, i, :], lambda i: wqkv[:, i, 512 * c:512 * c + 512]).then_inc(proj_done, 1)

            def transpose_qk(jt, i, n):
                c = (i % 2) * 2 + i // 2
                pe.wait_ge(qk_done, jt * 4 + i + 1)
                if i >= 2:
                    pe.wait_ge(qkT_done, jt * 4 + i - 1)
                elif n == 1:
                    pe.wait_ge(qkT_done, jt * 4 - 1 + i)
                elif n != 0 and i == 0:
                    pe.wait_ge(resid_done, jt - 1)
                elif n != 0:
                    pe.wait_ge(lv_done, jt - 1)
                for k in range(4):
                    last = nc.tensor.transpose(TR[i % 2][:, k * 128:(k + 1) * 128], uv[:, c, 0, k * 128:(k + 1) * 128], ident[:, :])
                last.then_inc(qkT_psum, 1)

            def scores(jt, g, first):
                pe.wait_ge(qkT_done, jt * 4 + 2 + 2 * (g // 2))
                if g >= 2 or not first:
                    pe.wait_ge(max_done, jt * 4 + g - 1)
                for k, h in enumerate(heads(g)):
                    r = slice(64 * (h % 2), 64 * (h % 2) + 64)
                    last = mm(SC[g % 2][:, k * 128:(k + 1) * 128], qT[r, h // 2, :], kT[r, h // 2, :])
                last.then_inc(score_done, 1)

            def transpose_prob(jt, g, first):
                pe.wait_ge(prob_done, jt * 4 + g + 1)
                if g or not first:
                    pe.wait_ge(probT_done, jt * 4 + g)
                for k in range(HG):
                    last = nc.tensor.transpose(PT[:, k * 128:(k + 1) * 128], prob[:, g % 2, k, :], ident[:, :])
                last.then_inc(probT_psum, 1)

            def times_v(jt, g, first):
                pe.wait_ge(probT_done, jt * 4 + g + 1)
                if g % 2 == 0:
                    pe.wait_ge(v_done, jt * 2 + 1 + g // 2)
                if g or not first:
                    pe.wait_ge(o_done, jt * 4 + g)
                for k, h in enumerate(heads(g)):
                    last = mm(OB[:, 65 * k:65 * k + 65], probT[:, g % 2, k, :], v[:, h, :])
                last.then_inc(av_done, 1)

            def transpose_o(kt, i, last_one):
                pe.wait_ge(o_done, kt * 4 + 2 * i + 2)
                if not last_one:
                    pe.wait_ge(qkT_done, kt * 4 + 7 + i)
                elif i == 0:
                    pe.wait_ge(resid_done, kt)
                else:
                    pe.wait_ge(lv_done, kt)
                for k in range(4):
                    c = 4 * i + k
                    last = nc.tensor.transpose(TR[i][:, k * 128:(k + 1) * 128],
                                               o[:, 2 * c:2 * c + 2, :].rearrange("p a b -> p (a b)"), ident[:, :])
                last.then_inc(oT_psum, 1)

            def out_project(kt):
                pe.wait_ge(oT_done, kt * 2 + 2)
                for c in range(8):
                    last = mm(TR[0][:, 0:128], wo[:, c, :], oT[:, c, :], c == 0, c == 7)
                last.then_inc(wo_done, 1)

            def attention(a, b, c, n=None):
                if a is not None:
                    project(a, 0, n == 0)
                if b is not None:
                    transpose_qk(b, 1, None if n is None else n - 1)
                if c is not None:
                    times_v(c, 3, n == 2)
                if b is not None:
                    transpose_qk(b, 2, None if n is None else n - 1)
                    scores(b, 0, n == 1)
                if a is not None:
                    project(a, 1, n == 0)
                if b is not None:
                    transpose_qk(b, 3, None if n is None else n - 1)
                    scores(b, 1, n == 1)
                if c is not None:
                    transpose_o(c, 0, b is None)
                if a is not None:
                    project(a, 2, n == 0)
                if c is not None:
                    transpose_o(c, 1, b is None)
                if a is not None:
                    project(a, 3, n == 0)
                if b is not None:
                    transpose_prob(b, 0, n == 1)
                    scores(b, 2, n == 1)
                    scores(b, 3, n == 1)
                    times_v(b, 0, n == 1)
                    transpose_prob(b, 1, n == 1)
                if c is not None:
                    out_project(c)
                if a is not None:
                    project(a, 4, n == 0)
                if b is not None:
                    transpose_prob(b, 2, n == 1)
                    times_v(b, 1, n == 1)
                if c is not None:
                    norm_mean(c)
                if b is not None:
                    transpose_prob(b, 3, n == 1)
                if a is not None:
                    project(a, 5, n == 0)
                if b is not None:
                    times_v(b, 2, n == 1)
                if c is not None:
                    norm_var(c)
                if a is not None:
                    transpose_qk(a, 0, n)

            def norm_mean(it):
                pe.wait_ge(sx_done, it * 2 + 2)
                pe.wait_ge(oT_done, it * 2 + 2)
                mm(TR[1][:, 0:N], mean_w[:, :], sx[:, :]).then_inc(mean_done, 1)

            def norm_var(it):
                pe.wait_ge(xq_done, it + 1)
                mm(TR[1][:, 0:N], mean_w[:, :], xq[:, :]).then_inc(var_done, 1)

            def ffn_up(k, kt, first):
                x_in = lambda i: xn[:, i, bass.ds(k * GB, GB), :].rearrange("p a b -> p (a b)")
                for j, (c0, w) in enumerate(FCH):
                    if not first:
                        pe.wait_ge(hid_raw_done, kt * 3 - 2 + j)
                    mm3(bank[2 * j][0:w, :], lambda i: w1[:, i, FI + c0:FI + c0 + w], x_in).then_inc(up_done, 1)
                    mm3(bank[2 * j + 1][0:w, :], lambda i: w1[:, i, c0:c0 + w], x_in).then_inc(up_done, 1)

            def ffn_down(kt, p, first):
                if not first:
                    pe.wait_ge(ffn_done, kt - 1)
                for j, (c0, w) in enumerate(FCH):
                    pe.wait_ge(hid_done, kt * 3 + 1 + j)
                    last = mm3(bank[6 + p][:, :], lambda i: w2[0:w, i, j, :], lambda i: hid[0:w, p, i, j, :], j == 0, j == 2)
                last.then_inc(down_done, 1)

            with pe.Fori(0, L) as l:
                pe.wait_ge(split_attn, l + 1)
                base = l * B
                attention(base, None, None, 0)
                attention(base + 1, base, None, 1)
                attention(base + 2, base + 1, base, 2)
                with pe.Fori(3, B) as n:
                    a = pe.snap(base + n)
                    attention(a, a - 1, a - 2)
                attention(None, base + (B - 1), base + (B - 2))
                attention(None, None, base + (B - 1))
                k0 = l * NG
                pe.wait_ge(xn_done, base + B)
                pe.wait_ge(split_ffn, l * 2 + 2)
                ffn_up(0, k0, True)
                ffn_up(1, k0 + 1, False)
                ffn_down(k0, 0, True)
                ffn_up(2, k0 + 2, False)
                ffn_down(k0 + 1, 1, True)
                with pe.Fori(1, NG // 2 - 1) as j:
                    for p in range(2):
                        k = pe.snap(j * 2 + p)
                        ffn_up(k + 1, k0 + k + 1, False)
                        ffn_down(k0 + k, p, False)
                ffn_up(NG - 1, k0 + (NG - 1), False)
                ffn_down(k0 + (NG - 2), 0, False)
                ffn_down(k0 + (NG - 1), 1, False)

            def result(k, p, first):
                pe.wait_ge(y_copy, k + 1)
                if not first:
                    pe.wait_ge(y_done, k - 1)
                for i in range(GB):
                    last = nc.tensor.transpose(PJ[p][:, i * 128:(i + 1) * 128], gate[:, p, 128 * i:128 * i + 128], ident[:, :])
                last.then_inc(y_psum, 1)

            result(0, 0, True)
            result(1, 1, True)
            with pe.Fori(1, NG // 2) as k:
                result(k * 2, 0, False)
                result(k * 2 + 1, 1, False)

        @block.scalar
        def _(act):
            nc.scalar.preload_act_table_set(EXP_LN)

            def c_values(n, first):
                act.wait_ge(c_vp, n + 1)
                if not first:
                    act.wait_ge(c_av, n * 4)
                    act.wait_ge(c_tail, n * 3)
                nc.scalar.copy(cv[:, :, 0:DC], TR[0][:, 0:128].rearrange("p (a b) -> p a b", a=HC)).then_inc(c_ve, 1)
                nc.scalar.copy(cvs[:, :, :].rearrange("p a b -> p (a b)"), TR[0][:, 128:256]).then_inc(c_ve, 1)

            def c_exp(m, g, first):
                act.wait_ge(c_max, m * 4 + g + 1)
                if g >= 2 or not first:
                    act.wait_ge(c_ptp, m * 4 + g - 1)
                for k in range(HG):
                    h = HG * g + k
                    last = nc.scalar.activation(prob[:, g % 2, k, :], SC[g % 2][:, k * 128:(k + 1) * 128], ACT.Exp,
                                                bias=cnm[:, h:h + 1])
                last.then_inc(c_prob, 1)

            def c_exp_self(m):
                act.wait_ge(c_ds, m + 1)
                nc.scalar.activation(eself[:, :], dself[:, :], ACT.Exp).then_inc(c_es, 1)

            def c_copy_probT(m, g, first):
                act.wait_ge(c_ptp, m * 4 + g + 1)
                if g >= 2 or not first:
                    act.wait_ge(c_av, m * 4 + g - 1)
                nc.scalar.copy(probT[:, g % 2, :, :].rearrange("p a b -> p (a b)"), PT[:, :]).then_inc(c_pt, 1)

            def c_iteration(m, first):
                c_exp(m, 0, first)
                c_exp(m, 1, first)
                c_values(m, first)
                c_copy_probT(m, 0, first)
                c_exp(m, 2, first)
                c_copy_probT(m, 1, first)
                c_exp(m, 3, first)
                c_copy_probT(m, 2, first)
                c_copy_probT(m, 3, first)
                c_exp_self(m)

            c_iteration(0, True)
            with act.Fori(1, B) as m:
                c_iteration(m, False)

            def copy_qkT(jt, i):
                act.wait_ge(qkT_psum, jt * 4 + i + 1)
                dst = (qT, kT)[i % 2]
                nc.scalar.copy(dst[:, 4 * (i // 2):4 * (i // 2) + 4, :].rearrange("p a b -> p (a b)"), TR[i % 2][:, :]).then_inc(qkT_done, 1)

            def square(it, c, first):
                act.wait_ge(proj_done, it * 6 + c + 1)
                if not first:
                    act.wait_ge(ss_done, it * 4 - 3 + c)
                nc.scalar.activation(sq[:, c, :], PJ[c % 2][:, :], ACT.Square).then_inc(sq_done, 1)

            def inverse_norms(it):
                act.wait_ge(ssm_done, it + 1)
                nc.scalar.activation(lnss[:, :], ssm[:, :], ACT.Ln).then_inc(ln_done, 1)
                act.wait_ge(ln_done, it + 1)
                nc.scalar.activation(rnorm[:, :], lnss[:, :], ACT.Exp, scale=-0.5).then_inc(rnorm_done, 1)

            def copy_v(it, c, first):
                act.wait_ge(proj_done, it * 6 + c + 1)
                if not first:
                    act.wait_ge(av_done, it * 4 - 10 + 2 * c)
                nc.scalar.copy(v[:, 8 * (c - 4):8 * (c - 4) + 8, 0:DH],
                               PJ[c % 2][:, :].rearrange("p (a b) -> p a b", a=8)).then_inc(v_done, 1)

            def exps(jt, g, first):
                act.wait_ge(max_done, jt * 4 + g + 1)
                if g >= 2 or not first:
                    act.wait_ge(probT_psum, jt * 4 + g - 1)
                for k in range(HG):
                    last = nc.scalar.activation(prob[:, g % 2, k, :], masked[:, g % 2, k, :], ACT.Exp,
                                                bias=nmax[:, g, k:k + 1], scale=-1.0)
                last.then_inc(prob_done, 1)

            def copy_oT(kt, i, first):
                act.wait_ge(oT_psum, kt * 2 + i + 1)
                if not first:
                    act.wait_ge(wo_done, kt)
                nc.scalar.copy(oT[:, 4 * i:4 * i + 4, :].rearrange("p a b -> p (a b)"), TR[i][:, :]).then_inc(oT_done, 1)

            def copy_probT(jt, g, first):
                act.wait_ge(probT_psum, jt * 4 + g + 1)
                if g >= 2 or not first:
                    act.wait_ge(av_done, jt * 4 + g - 1)
                nc.scalar.copy(probT[:, g % 2, :, :].rearrange("p a b -> p (a b)"), PT[:, :]).then_inc(probT_done, 1)

            def attention(a, b, c, n=None):
                if a is not None:
                    square(a, 0, n == 0)
                if b is not None:
                    copy_qkT(b, 1)
                    copy_v(b, 5, n == 1)
                    copy_qkT(b, 2)
                if a is not None:
                    square(a, 1, n == 0)
                if b is not None:
                    copy_qkT(b, 3)
                    exps(b, 0, n == 1)
                if c is not None:
                    copy_oT(c, 0, n == 2)
                if a is not None:
                    square(a, 2, n == 0)
                if b is not None:
                    copy_probT(b, 0, n == 1)
                    exps(b, 1, n == 1)
                if c is not None:
                    copy_oT(c, 1, n == 2)
                if a is not None:
                    square(a, 3, n == 0)
                if b is not None:
                    copy_probT(b, 1, n == 1)
                    exps(b, 2, n == 1)
                    exps(b, 3, n == 1)
                    copy_probT(b, 2, n == 1)
                if a is not None:
                    inverse_norms(a)
                if c is not None:
                    norm_square(c)
                if a is not None:
                    copy_v(a, 4, n == 0)
                if b is not None:
                    copy_probT(b, 3, n == 1)
                if c is not None:
                    norm_rstd(c)
                if a is not None:
                    copy_qkT(a, 0)

            def norm_square(it):
                act.wait_ge(xc_done, it + 1)
                nc.scalar.activation(xq[:, :], xc[:, :], ACT.Square).then_inc(xq_done, 1)

            def norm_rstd(it):
                act.wait_ge(var_done, it + 1)
                nc.scalar.activation(lv[:, :], TR[1][:, 0:N], ACT.Ln, bias=eps[:, :]).then_inc(lv_done, 1)
                act.wait_ge(lv_done, it + 1)
                nc.scalar.activation(rstd[:, :], lv[:, :], ACT.Exp, scale=-0.5).then_inc(rstd_done, 1)

            def ffn_gate(kt, first):
                for j, (c0, w) in enumerate(FCH):
                    act.wait_ge(up_done, kt * 6 + 2 * j + 1)
                    if not first:
                        act.wait_ge(hid_raw_done, kt * 3 - 2 + j)
                    nc.scalar.activation(gate[0:w, j, :], bank[2 * j][0:w, :], ACT.Gelu,
                                         bias=par[0:w, 3 + j:4 + j]).then_inc(gate_done, 1)

            def ffn_high(kt, p, two_before):
                for j, (c0, w) in enumerate(FCH):
                    act.wait_ge(hid_raw_done, kt * 3 + j + 1)
                    if two_before:
                        act.wait_ge(down_done, kt - 1)
                    nc.scalar.copy(hid[0:w, p, 0, j, :], hid_raw[0:w, j, :]).then_inc(hid_high, 1)

            with act.Fori(0, L) as l:
                nc.scalar.preload_act_table_set(EXP_LN)
                base = l * B
                attention(base, None, None, 0)
                attention(base + 1, base, None, 1)
                attention(base + 2, base + 1, base, 2)
                with act.Fori(3, B) as n:
                    a = act.snap(base + n)
                    attention(a, a - 1, a - 2)
                attention(None, base + (B - 1), base + (B - 2))
                attention(None, None, base + (B - 1))
                k0 = l * NG
                nc.scalar.preload_act_table(ACT.Gelu)
                act.wait_ge(ld_ffn, l * 64 + 64)
                ffn_gate(k0, True)
                ffn_high(k0, 0, False)
                ffn_gate(k0 + 1, False)
                ffn_high(k0 + 1, 1, False)
                with act.Fori(1, NG // 2) as j:
                    for p in range(2):
                        kt = act.snap(k0 + j * 2 + p)
                        ffn_gate(kt, False)
                        ffn_high(kt, p, True)

        @block.vector
        def _(dve):
            nc.vector.memset(one[:, :], 1.0).then_inc(const_dve, 1)
            nc.vector.memset(eps[:, :], 1e-5).then_inc(const_dve, 1)
            nc.vector.memset(resid[:, 0:B, 0:1], 0.0).then_inc(const_dve, 1)
            nc.vector.memset(v[:, :, DH:DH + 1], 1.0).then_inc(const_dve, 1)
            nc.vector.memset(cv[:, :, DC:DC + 1], 1.0).then_inc(const_dve, 1)
            nc.vector.memset(mean_w[:, :], 1.0 / D).then_inc(const_dve, 1)
            nc.vector.memset(ones_row[:, :], 1.0).then_inc(const_dve, 1)
            dve.wait_ge(ld_const, 80)
            dve.wait_ge(ld_cond, 176)
            nc.vector.tensor_copy(lenf[:, :], leni[:, :]).then_inc(const_dve, 1)
            dve.wait_ge(const_dve, 8)

            def c_copy_inputs(n, first):
                dve.wait_ge(c_tx, n + 1)
                if not first:
                    dve.wait_ge(c_vp, n)
                    dve.wait_ge(c_sbT, n)
                nc.vector.tensor_copy(sT[:, :, :].rearrange("p a b -> p (a b)"), PJ[0][:, 0:256]).then_inc(c_sT, 1)

            def c_bias_qk(n, first):
                dve.wait_ge(c_qk, n + 1)
                if not first:
                    dve.wait_ge(c_sc, n * 4)
                    dve.wait_ge(c_km, n)
                    dve.wait_ge(c_prod, n)
                nc.vector.tensor_scalar(cq[:, :], PJ[1][:, 0:128], cb[:, 0:1], DC ** -0.5, ALU.add, ALU.mult).then_inc(c_qke, 1)
                nc.vector.tensor_scalar(ck[:, :, :].rearrange("p a b -> p (a b)"), PJ[1][:, 128:384], cb[:, 1:2], None, ALU.add).then_inc(c_qke, 1)
                nc.vector.tensor_scalar(mrow[:, :, :].rearrange("p a b -> p (a b)"), iota4[:, :, :].rearrange("p a b -> p (a b)"),
                                        lenf[:, bass.ds(n, 1)], NEG, ALU.is_ge, ALU.mult).then_inc(c_mrow, 1)

            def c_negate_self(n, first):
                dve.wait_ge(c_self, n + 1)
                if not first:
                    dve.wait_ge(c_ds, n)
                nc.vector.tensor_scalar(nself[:, :], PJ[0][:, 256:256 + HC], -1.0, None, ALU.mult).then_inc(c_nself, 1)

            def c_group_max(m, g):
                dve.wait_ge(c_sc, m * 4 + g + 1)
                hs = slice(HG * g, HG * g + HG)
                nc.vector.tensor_reduce(cmax[:, hs], SC[g % 2][:, :].rearrange("p (a b) -> p a b", a=HG), AX.X, ALU.max,
                                        negate=True).then_inc(c_red, 1)
                dve.wait_ge(c_red, m * 4 + g + 1)
                dve.wait_ge(c_nself, m + 1)
                nc.vector.tensor_tensor(cnm[:, hs], cmax[:, hs], nself[:, hs], ALU.min).then_inc(c_max, 1)

            def c_self_difference(m):
                dve.wait_ge(c_max, m * 4 + 4)
                nc.vector.tensor_tensor(dself[:, :], cnm[:, :], nself[:, :], ALU.subtract).then_inc(c_ds, 1)

            def c_combine(m):
                ov = OB[:, 0:9 * HC].rearrange("p (a b) -> p a b", a=HC)
                dve.wait_ge(c_av, m * 4 + 4)
                dve.wait_ge(c_es, m + 1)
                dve.wait_ge(c_ve, m * 2 + 2)
                nc.vector.tensor_tensor(cden[:, :], ov[:, :, DC], eself[:, :], ALU.add).then_inc(c_tail, 1)
                nc.vector.tensor_tensor(cnum[:, :, :], cvs[:, :, :], eself[:, :].unsqueeze(2).to_broadcast([128, HC, DC]), ALU.mult).then_inc(c_tail, 1)
                dve.wait_ge(c_tail, m * 3 + 2)
                nc.vector.reciprocal(crd[:, :], cden[:, :]).then_inc(c_red2, 1)
                nc.vector.tensor_tensor(cnum2[:, :, :], cnum[:, :, :], ov[:, :, 0:DC], ALU.add).then_inc(c_tail, 1)
                dve.wait_ge(c_tail, m * 3 + 3)
                dve.wait_ge(c_red2, m + 1)
                nc.vector.tensor_tensor(att[:, :, :], cnum2[:, :, :], crd[:, :].unsqueeze(2).to_broadcast([128, HC, DC]), ALU.mult).then_inc(c_att, 1)

            def c_out_bias(m):
                dve.wait_ge(c_ta, m + 1)
                nc.vector.tensor_scalar(attT[:, :], TR[1][:, 0:128], cb[:, 2:3], None, ALU.add).then_inc(c_attT, 1)

            def c_write_resid(m):
                dve.wait_ge(c_wo, m + 1)
                nc.vector.tensor_scalar(resid[:, bass.ds(m, 1), 1:1 + N], TR[1][:, 128:256].unsqueeze(1), cb[:, 3:4], None, ALU.add).then_inc(c_out, 1)

            def c_iteration(a, b, c, n=None):
                if a is not None:
                    c_copy_inputs(a, n == 0)
                if b is not None:
                    c_group_max(b, 0)
                    c_group_max(b, 1)
                if c is not None:
                    c_combine(c)
                if b is not None:
                    c_group_max(b, 2)
                if a is not None:
                    c_bias_qk(a, n == 0)
                if c is not None:
                    c_out_bias(c)
                if b is not None:
                    c_group_max(b, 3)
                if c is not None:
                    c_write_resid(c)
                if b is not None:
                    c_self_difference(b)
                if a is not None:
                    c_negate_self(a, n == 0)

            c_iteration(0, None, None, 0)
            c_iteration(1, 0, None, 1)
            c_iteration(2, 1, 0, 2)
            with dve.Fori(3, B) as a:
                c_iteration(a, a - 1, a - 2)
            c_iteration(None, B - 1, B - 2)
            c_iteration(None, None, B - 1)

            def shift_xs(place, it, first):
                if not first:
                    dve.wait_ge(proj_done, it * 6)
                for half, off in ((0, 1), (1, 0)):
                    r = slice(64 * half, 64 * half + 64)
                    nc.vector.tensor_copy(xs[r, 0:1, :], resid[r, bass.ds(place, 1), off:off + N]).then_inc(xsh_done, 1)
                for half, off in ((0, 1), (1, 0)):
                    r = slice(64 * half, 64 * half + 64)
                    dve.wait_ge(xsh_done, it * 2 + half + 1)
                    nc.vector.tensor_tensor(xs[r, 1:2, :], resid[r, bass.ds(place, 1), off:off + N], xs[r, 0:1, :], ALU.subtract).then_inc(xs_done, 1)

            def rotate(it, c, first):
                dve.wait_ge(sq_done, it * 4 + c + 1)
                if not first:
                    dve.wait_ge(qkT_psum, it * 4 - 3 + (0, 2, 1, 3)[c])
                q = PJ[c % 2][:, :].rearrange("p (h d) -> p h d", h=8).unsqueeze(1).to_broadcast([128, 2, 8, DH])
                tb = tab[:, c // 2, :, :].unsqueeze(2).to_broadcast([128, 2, 8, DH])
                nc.vector.tensor_tensor(uv[:, c, :, :].rearrange("p a (h d) -> p a h d", h=8), q, tb, ALU.mult).then_inc(rot_done, 1)

            def sum_squares(it, c, first):
                dve.wait_ge(sq_done, it * 4 + c + 1)
                if c == 0 and not first:
                    dve.wait_ge(ssm_done, it)
                nc.vector.tensor_reduce(ss[:, 8 * c:8 * c + 8], sq[:, c, :].rearrange("p (h d) -> p h d", h=8), AX.X, ALU.add).then_inc(ss_done, 1)

            def clamp_squares(it, first):
                dve.wait_ge(ss_done, it * 4 + 4)
                if not first:
                    dve.wait_ge(ln_done, it)
                nc.vector.tensor_scalar(ssm[:, :], ss[:, :], 1e-24, None, ALU.max).then_inc(ssm_done, 1)

            def group_max(jt, g, first):
                dve.wait_ge(score_done, jt * 4 + g + 1)
                if g >= 2 or not first:
                    dve.wait_ge(prob_done, jt * 4 + g - 1)
                nc.vector.memset(held[:, g:g + 1], 0.0)
                for k in range(HG):
                    last = nc.vector.tensor_tensor_reduce(masked[:, g % 2, k, :], SC[g % 2][:, k * 128:(k + 1) * 128], maskf[:, :],
                                                          -1.0, -3.0 * NEG, ALU.add, ALU.min, nmax[:, g, k:k + 1])
                last.then_inc(max_done, 1)

            def normalise(jt, g, first):
                ov = OB[:, 0:65 * HG].rearrange("p (a b) -> p a b", a=HG)
                dve.wait_ge(av_done, jt * 4 + g + 1)
                nc.vector.reciprocal(rl[:, g, :], ov[:, :, DH]).then_inc(rl_done, 1)
                dve.wait_ge(rl_done, jt * 4 + g + 1)
                if g % 2 == 0 and not first:
                    dve.wait_ge(oT_psum, jt * 2 - 1 + g // 2)
                h0 = heads(g)[0]
                nc.vector.tensor_tensor(o[:, h0:h0 + 7:2, :], ov[:, :, 0:DH], rl[:, g, :].unsqueeze(2).to_broadcast([128, HG, DH]),
                                        ALU.mult).then_inc(o_done, 1)

            def add_resid(k, kt):
                dve.wait_ge(wo_done, kt + 1)
                r = resid[:, bass.ds(k, 1), 1:1 + N]
                nc.vector.tensor_tensor(r, TR[0][:, 0:128].unsqueeze(1), r, ALU.add).then_inc(resid_done, 1)

            def attention(place, a, b, c, d, n=None):
                if a is not None:
                    shift_xs(place, a, n == 0)
                if c is not None:
                    normalise(c, 2, n == 2)
                if d is not None:
                    norm_finish(place - 3, d, n == 3)
                if a is not None:
                    rotate(a, 0, n == 0)
                if c is not None:
                    normalise(c, 3, n == 2)
                if b is not None:
                    group_max(b, 0, n == 1)
                if a is not None:
                    sum_squares(a, 0, n == 0)
                    rotate(a, 1, n == 0)
                if b is not None:
                    group_max(b, 1, n == 1)
                if a is not None:
                    rotate(a, 2, n == 0)
                    sum_squares(a, 1, n == 0)
                    sum_squares(a, 2, n == 0)
                if b is not None:
                    group_max(b, 2, n == 1)
                    normalise(b, 0, n == 1)
                    group_max(b, 3, n == 1)
                if a is not None:
                    sum_squares(a, 3, n == 0)
                if c is not None:
                    add_resid(place - 2, c)
                if a is not None:
                    clamp_squares(a, n == 0)
                if c is not None:
                    norm_center(place - 2, c, n == 2)
                if a is not None:
                    rotate(a, 3, n == 0)
                if b is not None:
                    normalise(b, 1, n == 1)
                if c is not None:
                    norm_subtract(c, n == 2)

            def norm_center(place, it, first):
                dve.wait_ge(resid_done, it + 1)
                if not first:
                    dve.wait_ge(xc_done, it)
                for half, off in ((0, 1), (1, 0)):
                    h = slice(64 * half, 64 * half + 64)
                    nc.vector.tensor_scalar(sx[h, :].unsqueeze(1), resid[h, bass.ds(place, 1), off:off + N], 1.0, None, ALU.mult).then_inc(sx_done, 1)

            def norm_subtract(it, first):
                dve.wait_ge(mean_done, it + 1)
                dve.wait_ge(sx_done, it * 2 + 2)
                if not first:
                    dve.wait_ge(xg_done, it)
                nc.vector.tensor_tensor(xc[:, :], sx[:, :], TR[1][:, 0:N], ALU.subtract).then_inc(xc_done, 1)

            def norm_finish(place, it, first):
                dve.wait_ge(rstd_done, it + 1)
                if not first:
                    dve.wait_ge(xn_done, it)
                nc.vector.scalar_tensor_tensor(out=xg[:, :], in0=xc[:, :], scalar=par[:, 7:8], in1=rstd[:, :],
                                               op0=ALU.mult, op1=ALU.mult).then_inc(xg_done, 1)
                dve.wait_ge(xg_done, it + 1)
                x = xg[:, :].unsqueeze(1)
                nc.vector.tensor_scalar(xn[:, 0, bass.ds(place, 1), :], x, par[:, 8:9], None, ALU.add).then_inc(xnh_done, 1)
                dve.wait_ge(xnh_done, it + 1)
                nc.vector.scalar_tensor_tensor(out=xn[:, 1, bass.ds(place, 1), :], in0=x, scalar=par[:, 8:9], in1=xn[:, 0, bass.ds(place, 1), :],
                                               op0=ALU.add, op1=ALU.subtract).then_inc(xn_done, 1)

            def ffn_hidden(kt, p, first):
                for j, (c0, w) in enumerate(FCH):
                    dve.wait_ge(up_done, kt * 6 + 2 * j + 2)
                    dve.wait_ge(gate_done, kt * 3 + j + 1)
                    if not first:
                        dve.wait_ge(hid_done, kt * 3 - 2 + j)
                    nc.vector.scalar_tensor_tensor(out=hid_raw[0:w, j, :], in0=bank[2 * j + 1][0:w, :], scalar=par[0:w, j:j + 1],
                                                   in1=gate[0:w, j, :], op0=ALU.add, op1=ALU.mult).then_inc(hid_raw_done, 1)
                    if j:
                        ffn_low(kt, p, j - 1)
                ffn_low(kt, p, 2)

            def ffn_low(kt, p, j):
                w = FCH[j][1]
                dve.wait_ge(hid_high, kt * 3 + j + 1)
                nc.vector.tensor_tensor(hid[0:w, p, 1, j, :], hid_raw[0:w, j, :], hid[0:w, p, 0, j, :], ALU.subtract).then_inc(hid_done, 1)

            def ffn_resid(k, kt, p):
                dve.wait_ge(down_done, kt + 1)
                r = resid[:, bass.ds(k * GB, GB), 1:1 + N]
                nc.vector.scalar_tensor_tensor(out=r, in0=bank[6 + p][:, :].rearrange("p (a b) -> p a b", a=GB), scalar=par[:, 6:7],
                                               in1=r, op0=ALU.add, op1=ALU.add).then_inc(ffn_done, 1)

            with dve.Fori(0, L) as l:
                dve.wait_ge(ld_attn, l * 64 + 64)
                for i in range(2):
                    nc.vector.tensor_tensor(tab[:, i, :, :], rot[:, i, :, :], scl[:, i, :].unsqueeze(1).to_broadcast([128, 2, DH]),
                                            ALU.mult).then_inc(tab_done, 1)
                dve.wait_ge(tab_done, l * 2 + 2)
                base = l * B
                attention(0, base, None, None, None, 0)
                attention(1, base + 1, base, None, None, 1)
                attention(2, base + 2, base + 1, base, None, 2)
                dve.wait_ge(ld_ffn, l * 64 + 64)
                attention(3, base + 3, base + 2, base + 1, base, 3)
                with dve.Fori(4, B) as n:
                    a = dve.snap(base + n)
                    attention(n, a, a - 1, a - 2, a - 3)
                attention(B, None, base + (B - 1), base + (B - 2), base + (B - 3))
                attention(B + 1, None, None, base + (B - 1), base + (B - 2))
                attention(B + 2, None, None, None, base + (B - 1))
                k0 = l * NG
                ffn_hidden(k0, 0, True)
                ffn_hidden(k0 + 1, 1, False)
                ffn_resid(0, k0, 0)
                with dve.Fori(1, NG // 2) as j:
                    for p in range(2):
                        k = dve.snap(j * 2 + p)
                        ffn_hidden(k0 + k, p, False)
                        ffn_resid(k - 1, k0 + k - 1, 1 - p)
                ffn_resid(NG - 1, k0 + (NG - 1), 1)
                dve.wait_ge(ffn_done, l * NG + NG)

            def result(k, p, first):
                if not first:
                    dve.wait_ge(y_psum, k - 1)
                nc.vector.tensor_copy(gate[:, p, :].rearrange("p (a b) -> p a b", a=GB), resid[:, bass.ds(k * GB, GB), 1:1 + N]).then_inc(y_copy, 1)

            def result_sum(k, p):
                dve.wait_ge(y_psum, k + 1)
                y = xall[:, bass.ds(k * GB, GB), :]
                nc.vector.tensor_tensor(y, PJ[p][:, :].rearrange("p (a b) -> p a b", a=GB), y, ALU.add).then_inc(y_done, 1)

            result(0, 0, True)
            result(1, 1, True)
            dve.wait_ge(y_load, 16)
            result_sum(0, 0)
            result_sum(1, 1)
            with dve.Fori(1, NG // 2) as k:
                for p in range(2):
                    result(k * 2 + p, p, False)
                for p in range(2):
                    result_sum(k * 2 + p, p)

        @block.gpsimd
        def _(po):
            po.wait_ge(ld_const, 80)
            po.wait_ge(ld_cond, 176)
            po.wait_ge(const_dve, 8)

            def c_bias(n, first):
                po.wait_ge(c_sT, n + 1)
                if not first:
                    po.wait_ge(c_qk, n)
                nc.gpsimd.tensor_tensor(sbT[:, :, :], sT[:, :, :], cb[:, 4:6].unsqueeze(2).to_broadcast([128, 2, 128]), ALU.add).then_inc(c_sbT, 1)

            def c_keys(n, first):
                po.wait_ge(c_qke, n * 2 + 2)
                if not first:
                    po.wait_ge(c_self, n)
                nc.gpsimd.tensor_tensor(qk_self[:, :], cq[:, :], ck[:, 1, :], ALU.mult).then_inc(c_prod, 1)
                if not first:
                    po.wait_ge(c_sc, n * 4)
                nc.gpsimd.tensor_tensor(km[:, :, :], ck[:, 0, :].unsqueeze(1).to_broadcast([128, HC, 128]),
                                        hsel[:, :].unsqueeze(2).to_broadcast([128, HC, 128]), ALU.mult).then_inc(c_km, 1)

            c_bias(0, True)
            c_keys(0, True)
            with po.Fori(1, B) as n:
                c_bias(n, False)
                c_keys(n, False)

            def finish_qk(it, first):
                def add(c):
                    po.wait_ge(rot_done, it * 4 + c + 1)
                    u = uv[:, c, 0, :].rearrange("p (h s d) -> p h s d", h=8, s=2)
                    w = uv[:, c, 1, :].rearrange("p (h s d) -> p h s d", h=8, s=2)
                    nc.gpsimd.tensor_tensor(u, u, w[:, :, ::-1, :], ALU.add).then_inc(add_done, 1)

                def times_norm(c):
                    po.wait_ge(add_done, it * 4 + c + 1)
                    u = uv[:, c, 0, :].rearrange("p (h d) -> p h d", h=8)
                    nc.gpsimd.tensor_tensor(u, u, rnorm[:, 8 * c:8 * c + 8].unsqueeze(2).to_broadcast([128, 8, DH]), ALU.mult).then_inc(qk_done, 1)

                for c in (0, 1, 2):
                    add(c)
                po.wait_ge(rnorm_done, it + 1)
                for c in (0, 2, 1):
                    times_norm(c)
                add(3)
                times_norm(3)

            def split(dst, raw, done, before, shape):
                nc.gpsimd.tensor_tensor(dst(0), raw, shape(one[:, :]), ALU.mult).then_inc(split_high, 1)
                po.wait_ge(split_high, before + 1)
                nc.gpsimd.tensor_tensor(dst(1), raw, dst(0), ALU.subtract).then_inc(done, 1)

            def split_attention(l):
                po.wait_ge(ld_attn, l * 64 + 64)
                split(lambda i: wqkv[:, i, :], wqkv_raw, split_attn, l * 4, lambda a: a.to_broadcast([128, 3 * INNER]))

            def split_feedforward(l):
                po.wait_ge(ld_ffn, l * 64 + 64)
                split(lambda i: w1[:, i, :], w1_raw[:, :], split_ffn, l * 4 + 1, lambda a: a.to_broadcast([128, 2 * FI]))
                split(lambda i: w2[:, i, 0:2, :], w2_raw[:, 0:2, :], split_ffn0, l * 4 + 2, lambda a: a.unsqueeze(2).to_broadcast([128, 2, D]))
                split(lambda i: w2[0:FI - 256, i, 2, :], w2_raw[0:FI - 256, 2, :], split_ffn, l * 4 + 3,
                      lambda a: a[0:FI - 256, :].to_broadcast([FI - 256, D]))

            split_attention(0)
            with po.Fori(0, L - 1) as l:
                with po.Fori(0, B) as n:
                    finish_qk(l * B + n, False)
                split_feedforward(l)
                split_attention(l + 1)
            with po.Fori(0, B) as n:
                finish_qk((L - 1) * B + n, False)
            split_feedforward(L - 1)


def _constants(N, DH, HC, D):
    import numpy as np
    f = np.float32
    i, j = np.arange(N)[:, None], np.arange(N)[None, :]
    mask = np.where((j > i) | (i > j + 32), f(NEG), f(0)).astype(f)
    half = np.arange(0, DH, 2, dtype=f)
    inv_freq = (f(1.0) / f(10000.0) ** (half / f(DH))).astype(f)
    tt = np.arange(N, dtype=f)
    freqs = (tt[:, None] * inv_freq[None, :]).astype(f)
    base = (half + f(0.4 * DH)) / f(1.4 * DH)
    power = (tt - N // 2) / f(16)
    scale = (base[None, :] ** power[:, None]).astype(f)
    cos, sin = np.cos(freqs).astype(f), np.sin(freqs).astype(f)
    two = lambda a, b: np.concatenate([a, b], -1)
    rot = np.zeros((N, 2, 2, DH), f)
    rot[:, 0, 0] = two(cos * scale, cos * scale) * f(8)
    rot[:, 0, 1] = two(sin * scale, -sin * scale) * f(8)
    rot[:, 1, 0] = two(cos / scale, cos / scale)
    rot[:, 1, 1] = two(sin / scale, -sin / scale)
    hsel = (np.arange(D)[:, None] // (D // HC) == np.arange(HC)[None, :]).astype(f)
    iota = np.tile(np.arange(N, dtype=f), 4).reshape(1, 4, N)
    return {"c_ident": np.eye(128, dtype=f), "c_mask": mask, "c_rot": rot, "c_hsel": hsel, "c_iota": iota}


def kernel(**inputs):
    import numpy as np
    import concourse.bacc as _bacc
    from concourse import mybir as _mybir
    from concourse.bass_utils import run_bass_kernel_spmd as _run

    a = {k: np.asarray(w) for k, w in inputs.items()}
    col = lambda w: np.ascontiguousarray(w).reshape(-1, 1)
    arrays = {
        "x": a["x"], "fside": a["fside_BxSxS_0"], "seq_len": a["itok_B_18_1004"].reshape(1, -1),
        "cWq": a["L0_cond_Wq"], "cWk": a["L0_cond_Wk"], "cWv": a["L0_cond_Wv"], "cWo": a["L0_cond_Wo"],
        "cbq": col(a["L0_cond_bq"]), "cbk": col(a["L0_cond_bk"]), "cbv": col(a["L0_cond_bv"]), "cbo": col(a["L0_cond_bo"]),
        "b_prev": col(a["L0_cond_b_prev"]), "b_self": col(a["L0_cond_b_self"]),
        "Wqkv": a["L0_ffn_Wqkv"], "q_scale": a["L0_ffn_q_scale"], "k_scale": a["L0_ffn_k_scale"], "Wo": a["L0_ffn_Wo"],
        "W1": a["L0_ffn_W1"], "W2": a["L0_ffn_W2"],
    }
    b1, b2 = a["L0_ffn_b1"], a["L0_ffn_b2"]
    L, FI = b1.shape[0], b1.shape[1] // 2
    par = np.zeros((L, 128, 9), b1.dtype)
    for half in range(2):
        for j, c in enumerate(range(0, FI, 128)):
            w = min(128, FI - c)
            par[:, :w, 3 * half + j] = b1[:, half * FI + c:half * FI + c + w]
    par[:, :, 6], par[:, :, 7], par[:, :, 8] = b2, a["L0_ffn_ln_g"], a["L0_ffn_ln_b"]
    arrays["par"] = par
    arrays.update(_constants(128, 64, 16, 128))
    arrays = {k: np.ascontiguousarray(w) for k, w in arrays.items()}
    nc = _bacc.Bacc("TRN2", target_bir_lowering=False, num_devices=1)
    t = {k: nc.dram_tensor(f"in_{k}", w.shape, _mybir.dt.from_np(w.dtype), kind="ExternalInput").ap() for k, w in arrays.items()}
    t["out"] = nc.dram_tensor("out", a["x"].shape, _mybir.dt.from_np(a["x"].dtype), kind="ExternalOutput").ap()
    build(nc, t)
    r = _run(nc, [{f"in_{k}": w for k, w in arrays.items()}], core_ids=[0])
    return r.results[0]["out"]
```
